# Optimizing a Trainium2 kernel written in Bass

```python
import numpy as np
import jax
import jax.numpy as jnp

def _softmax(x, axis=-1):
    return jax.nn.softmax(x, axis=axis)

def _gelu(x):
    return jax.nn.gelu(x, approximate=True)

def _silu(x):
    return jax.nn.silu(x)

def _sigmoid(x):
    return jax.nn.sigmoid(x)

def _layernorm(x, axis=-1, eps=1e-05):
    m = jnp.mean(x, axis=axis, keepdims=True)
    v = jnp.var(x, axis=axis, keepdims=True)
    return (x - m) / jnp.sqrt(v + eps)

def _scatter_add(tgt, idx, src, axis=0):
    return tgt.at[idx].add(src)

def _segment_sum(src, seg, n):
    return jax.ops.segment_sum(src, seg, n)
kernel_name = 'mk_adaln_ffn_d1_seqx_r4_333706'

def setup_inputs(seed: int=0):
    np.random.seed(seed)
    _w = jnp.asarray

    def _rec_inputs():
        import jax
        import jax.numpy as jnp
        _rk = jax.random.key(seed)
        x = -0.0002928 + 1 * jax.random.normal(jax.random.fold_in(_rk, 1), (8, 512, 256), jnp.float32)
        _lenS = 512 - jax.random.randint(jax.random.fold_in(_rk, 7), (8,), 0, max(1, 512 // 4) + 1, jnp.int32)
        _lenS2 = 512 - jax.random.randint(jax.random.fold_in(_rk, 8), (8,), 0, max(1, 512 // 4) + 1, jnp.int32)
        fside_16xSxS_0 = -5.72187e-05 + 0.999849 * jax.random.normal(jax.random.fold_in(_rk, 11), (16, 512, 512), jnp.float32)
        cond_64 = -0.0265395 + 0.99382 * jax.random.normal(jax.random.fold_in(_rk, 13), (8, 64), jnp.float32)
        _validS = jnp.arange(512)[None, :] < _lenS[:, None]
        _validS2 = jnp.arange(512)[None, :] < _lenS2[:, None]
        _causal = jnp.tril(jnp.ones((512, 512), dtype=bool))
        mask_BxS_bk0 = jnp.logical_not(jnp.broadcast_to(_validS[:, :], (8, 512)))
        return (x, fside_16xSxS_0, cond_64, mask_BxS_bk0)
    x, fside_16xSxS_0, cond_64, mask_BxS_bk0 = _rec_inputs()

    def _L0_cond_setup():
        import jax, jax.numpy as jnp
        import numpy as np
        B, N, DIM, H, DH = (2, 512, 256, 16, 64)
        INNER = H * DH
        EPS = 1e-05

        def layernorm(x, g):
            mean = jnp.mean(x, axis=-1, keepdims=True)
            var = jnp.var(x, axis=-1, keepdims=True)
            return (x - mean) * jax.lax.rsqrt(var + EPS) * g
        key = jax.random.key(seed)
        ks = jax.random.split(key, 10)
        x = jax.random.normal(ks[0], (B, N, DIM), dtype=jnp.float32)
        attn_bias = jax.random.normal(ks[1], (H, N, N), dtype=jnp.float32)
        mask = jax.random.randint(ks[2], (B, N), 0, 2).astype(bool)
        g_in = jnp.ones((DIM,), dtype=jnp.float32)
        null_attn_bias = jax.random.normal(ks[3], (H,), dtype=jnp.float32)
        null_kv = jax.random.normal(ks[4], (2, DH), dtype=jnp.float32)
        Wq = jax.random.normal(ks[5], (DIM, INNER), dtype=jnp.float32) * 0.02
        Wkv = jax.random.normal(ks[6], (DIM, 2 * DH), dtype=jnp.float32) * 0.02
        Wo = jax.random.normal(ks[7], (INNER, DIM), dtype=jnp.float32) * 0.02
        g_out = jnp.ones((DIM,), dtype=jnp.float32)
        return {'x': x, 'attn_bias': attn_bias, 'mask': mask, 'g_in': g_in, 'null_attn_bias': null_attn_bias, 'null_kv': null_kv, 'Wq': Wq, 'Wkv': Wkv, 'Wo': Wo, 'g_out': g_out}
    _L0_cond_all = _L0_cond_setup()
    _L0_cond_in = {k: v for k, v in _L0_cond_all.items() if k in ('g_in', 'null_attn_bias', 'Wq', 'Wkv', 'Wo', 'g_out')}
    del _L0_cond_all

    def _L0_ffn_setup():
        import jax, jax.numpy as jnp
        import numpy as np
        key = jax.random.key(seed)
        ks = jax.random.split(key, 5)
        B, S, D_in, D_out, E, R = (4, 256, 256, 256, 8, 16)
        x = jax.random.normal(ks[0], (B, S, D_in), dtype=jnp.float32)
        weight = jax.random.normal(ks[1], (D_out, D_in), dtype=jnp.float32) / np.sqrt(D_in)
        gate_w = jax.random.normal(ks[2], (E, D_in), dtype=jnp.float32) / np.sqrt(D_in)
        lora_U = jax.random.normal(ks[3], (E, R, D_in), dtype=jnp.float32) / np.sqrt(D_in)
        lora_V = jax.random.normal(ks[4], (E, D_out, R), dtype=jnp.float32) / np.sqrt(R)
        return {'x': x, 'weight': weight, 'gate_w': gate_w, 'lora_U': lora_U, 'lora_V': lora_V}
    _L0_ffn_all = _L0_ffn_setup()
    _L0_ffn_in = {k: v for k, v in _L0_ffn_all.items() if k in ('weight', 'gate_w', 'lora_U', 'lora_V')}
    del _L0_ffn_all
    return {'x': x, 'fside_16xSxS_0': fside_16xSxS_0, 'cond_64': cond_64, 'mask_BxS_bk0': mask_BxS_bk0, 'L0_cond_g_in': _L0_cond_in['g_in'], 'L0_cond_null_attn_bias': _L0_cond_in['null_attn_bias'], 'L0_cond_Wq': _L0_cond_in['Wq'], 'L0_cond_Wkv': _L0_cond_in['Wkv'], 'L0_cond_Wo': _L0_cond_in['Wo'], 'L0_cond_g_out': _L0_cond_in['g_out'], 'L0_ffn_weight': _L0_ffn_in['weight'], 'L0_ffn_gate_w': _L0_ffn_in['gate_w'], 'L0_ffn_lora_U': _L0_ffn_in['lora_U'], 'L0_ffn_lora_V': _L0_ffn_in['lora_V']}

def reference(x, fside_16xSxS_0, cond_64, mask_BxS_bk0, L0_cond_g_in, L0_cond_null_attn_bias, L0_cond_Wq, L0_cond_Wkv, L0_cond_Wo, L0_cond_g_out, L0_ffn_weight, L0_ffn_gate_w, L0_ffn_lora_U, L0_ffn_lora_V):
    import jax
    import jax.numpy as jnp

    def _L0_cond_ref(x, attn_bias, mask, g_in, null_attn_bias, null_kv, Wq, Wkv, Wo, g_out):
        import jax, jax.numpy as jnp
        import numpy as np
        B, N, DIM, H, DH = (2, 512, 256, 16, 64)
        INNER = H * DH
        EPS = 1e-05

        def layernorm(x, g):
            mean = jnp.mean(x, axis=-1, keepdims=True)
            var = jnp.var(x, axis=-1, keepdims=True)
            return (x - mean) * jax.lax.rsqrt(var + EPS) * g
        b, n, _ = x.shape
        scale = DH ** (-0.5)
        xn = layernorm(x, g_in)
        q = (xn @ Wq).reshape(b, n, H, DH).transpose(0, 2, 1, 3) * scale
        kv = xn @ Wkv
        k, v = (kv[..., :DH], kv[..., DH:])
        nk = jnp.broadcast_to(null_kv[0], (b, 1, DH))
        nv = jnp.broadcast_to(null_kv[1], (b, 1, DH))
        k = jnp.concatenate([nk, k], axis=1)
        v = jnp.concatenate([nv, v], axis=1)
        sim = jnp.einsum('bhid,bjd->bhij', q, k)
        null_col = jnp.broadcast_to(null_attn_bias[:, None, None], (H, n, 1))
        bias = jnp.concatenate([null_col, attn_bias], axis=-1)
        sim = sim + bias
        neg = -jnp.finfo(sim.dtype).max
        j = n + 1
        causal_mask = jnp.triu(jnp.ones((n, j), dtype=bool), k=j - n + 1)
        sim = jnp.where(causal_mask, neg, sim)
        mask_p = jnp.pad(mask, ((0, 0), (1, 0)), constant_values=True)
        sim = jnp.where(mask_p[:, None, None, :], sim, neg)
        attn = jax.nn.softmax(sim, axis=-1)
        out = jnp.einsum('bhij,bjd->bhid', attn, v)
        out = out.transpose(0, 2, 1, 3).reshape(b, n, INNER)
        out = out @ Wo
        return layernorm(out, g_out)

    def _L0_ffn_ref(x, weight, gate_w, lora_U, lora_V):
        import jax, jax.numpy as jnp
        import numpy as np
        scaling = 1.0 / lora_U.shape[1]
        B, S, D_in = x.shape
        xt = x.reshape(-1, D_in)
        gate = jax.nn.softmax(xt @ gate_w.T, axis=-1)
        base = xt @ weight.T
        t = jnp.einsum('nh,erh->ner', xt, lora_U)
        lora = jnp.einsum('ne,eor,ner->no', gate, lora_V, t)
        out = base + scaling * lora
        return out.reshape(B, S, -1)
    x = x + _L0_ffn_ref(_L0_cond_ref(x, fside_16xSxS_0, mask_BxS_bk0, L0_cond_g_in, L0_cond_null_attn_bias, cond_64, L0_cond_Wq, L0_cond_Wkv, L0_cond_Wo, L0_cond_g_out), L0_ffn_weight, L0_ffn_gate_w, L0_ffn_lora_U, L0_ffn_lora_V)
    return x

_drawn_inputs = setup_inputs


def setup_inputs(seed=0):
    import zlib

    import numpy as np

    out = dict(_drawn_inputs(seed))
    spreads = {'L0_cond_g_in': (1.0, 0.2), 'L0_cond_g_out': (1.0, 0.2)}
    factors = {}
    for name, (base, spread) in spreads.items():
        noise = np.random.default_rng([zlib.crc32(name.encode()), seed]).standard_normal(out[name].shape)
        drawn = base * np.exp(spread * noise) if base else spread * noise
        out[name] = jnp.asarray(drawn.astype(out[name].dtype))
    for name, factor in factors.items():
        out[name] = (out[name] * factor).astype(out[name].dtype)
    return out
```

```python
from contextlib import ExitStack

import concourse.bass as bass
from concourse import mybir

ALU = mybir.AluOpType
ACT = mybir.ActivationFunctionType
AX = mybir.AxisListType
F32 = mybir.dt.float32
BF16 = mybir.dt.bfloat16
U8 = mybir.dt.uint8
I32 = mybir.dt.int32

P = 128
B, N, D = 8, 512, 256
H, DH = 16, 64
INNER = H * DH
DC = D // P
MC = INNER // P
QT = N // P
E, R = 8, 16
EPS = 1e-5
SCALE = DH ** -0.5
FAR = 1e30
FW = D + E * R + E
PART = 4
TAIL = ((0, "out"), (1, "norm"), (2, "ffn"), (2, "gate"), (3, "lora"), (3, "store"))


class Layout:

    def __init__(self, late):
        self.late = late
        self.rounds = 1 if late else B
        self.preps = 2 if late else 1
        self.tiles = PART * self.preps
        self.nk = [P if late else P * (t + 1) for t in range(self.tiles)]
        self.k0 = [P * (t % PART) if late else 0 for t in range(self.tiles)]
        self.units = []
        for t in range(self.tiles):
            per = {P: 4, 2 * P: 2}.get(self.nk[t], 1)
            self.units += [(t, h, per) for h in range(0, H, per)]
        self.nu = len(self.units)
        self.first_side = 1 if late else 0
        self.sides = self.tiles + self.first_side
        last = {}
        for u, (t, h, per) in enumerate(self.units):
            last[t, h // 8] = u + 3
        self.side = {}

        def put(step, piece):
            self.side.setdefault(step, []).append(piece)

        if late:
            for k, name in TAIL:
                put(k, (name, -1, 0))
        for t in range(self.tiles):
            for hf in range(2):
                put(last[t, hf] - 1, ("den", t, hf))
                put(last[t, hf], ("ctx", t, hf))
                put(last[t, hf] + 1, ("turn", t, hf))
            for k, name in TAIL:
                put(last[t, 1] + 2 + k, (name, t, 0))
        self.steps = max(self.side) + 1
        order = ["out", "norm", "ffn", "gate", "lora", "store", "den", "ctx", "turn"]
        for pieces in self.side.values():
            pieces.sort(key=lambda x: (x[1], order.index(x[0]), x[2]))


def attention_ffn(nc, x_d, bias_d, cond_d, mask_d, g_in_d, nb_d, wq_d, wkv_d, wo_d, g_out_d,
                  w_d, gate_d, u_d, v_d, out_d):
    ctx = ExitStack()
    with ctx:
        def sb(name, shape, dt=F32):
            return ctx.enter_context(nc.sbuf_tensor(name, shape, dt))

        def bank(name):
            return ctx.enter_context(nc.psum_tensor(name, [P, 512], F32))

        def sem(name):
            return ctx.enter_context(nc.semaphore(name))

        x_all = sb("x_all", [P, B, QT, D])
        ident = sb("ident", [P, P])
        wq = sb("wq", [P, DC, INNER])
        wkk = sb("wkk", [P, DC, P])
        wvn = sb("wvn", [P, DC, DH + H])
        wo = sb("wo", [P, MC, D])
        wcat = sb("wcat", [P, DC, FW])
        vcat = sb("vcat", [P, D])
        g_in = sb("g_in", [P, DC])
        g_out = sb("g_out", [P, DC])
        null_k = sb("null_k", [P, DH])
        null_v = sb("null_v", [P, DH])
        null_vt = sb("null_vt", [P, 1])
        null_ctx = sb("null_ctx", [P, P])
        null_bias = sb("null_bias", [P, H])
        y_null = sb("y_null", [P, D])
        pick = sb("pick", [P, P], BF16)
        mask_far = sb("mask_far", [P, B, N], BF16)
        xn = sb("xn", [P, PART, D])
        xn_t = sb("xn_t", [P, DC, N])
        q_all = sb("q_all", [P, MC, N])
        kt_all = sb("kt_all", [P, 2, N])
        v_all = sb("v_all", [P, 2, PART, DH])
        ns_all = sb("ns_all", [P, 2, PART, H])
        scores = sb("scores", [P, 3, 512])
        probs = sb("probs", [P, 3, 512])
        probs_t = sb("probs_t", [P, 2, 512])
        attn = sb("attn", [P, 2, 512])
        null_part = sb("null_part", [P, 2, 512])
        attn_t = sb("attn_t", [P, MC, P])
        xt = sb("xt", [P, D])
        xt_t = sb("xt_t", [P, DC, P])
        tg = sb("tg", [P, E * R])
        tg_t = sb("tg_t", [P, P])
        stat = sb("stat", [P, PART, 6])
        mv = sb("mv", [P, PART, 2])
        rstd = sb("rstd", [P, PART])
        half = sb("half", [P, PART])
        neg_max = sb("neg_max", [P, 2, H])
        sums = sb("sums", [P, 2, H])
        small = sb("small", [P, 5, 2, 8])
        ostat = sb("ostat", [P, 6])
        omv = sb("omv", [P, 2])
        orstd = sb("orstd", [P, 1])
        flag_f = sb("flag_f", [P, 1])
        flag = sb("flag", [P, 1], I32)
        gate_s = sb("gate_s", [P, 4, E])
        big = sb("big", [P, H * P * (1 + 2 + 3 + 4)])
        starts = [0, H * P, 3 * H * P, 6 * H * P]
        bias_all = [big[:, s:s + H * P * (j + 1)].rearrange("p (h k) -> p h k", h=H)
                    for j, s in enumerate(starts)]
        o = [0]

        def carve(n):
            o[0] += n
            return big[:, o[0] - n:o[0]]

        bias_late = carve(H * P).rearrange("p (h k) -> p h k", h=H)
        q_late = carve(MC * N).rearrange("p (m n) -> p m n", m=MC)
        kt_late = carve(2 * N).rearrange("p (e n) -> p e n", e=2)
        w_raw = carve(2 * D).rearrange("p (o d) -> p o d", o=2)
        u_raw = carve(D)
        gate_raw = carve(D)
        v_raw = carve(2 * E * R).rearrange("p (o n) -> p o n", o=2)
        wkv_raw = carve(DC * P).rearrange("p (c n) -> p c n", c=DC)
        wqk = carve(DC * INNER).rearrange("p (c h e) -> p c h e", c=DC, h=H)
        mask_room = carve(B * N // 4)
        mask_raw = mask_room.bitcast(U8).rearrange("p (b n) -> p b n", b=B)
        mask_words = mask_room.bitcast(I32).rearrange("p (b n) -> p b n", b=B)

        s_bank = [bank("s_bank0"), bank("s_bank1")]
        t_bank = [bank("t_bank0"), bank("t_bank1")]
        c_bank = [bank("c_bank0"), bank("c_bank1")]
        x_bank = bank("x_bank")
        m_bank = bank("m_bank")
        q_banks = s_bank + t_bank

        NAMES = """x_late_in x_rest_in wq_in wkv_in small_in mask_in bias_in bias_in0 bias_in1 bias_in2 bias_in3 wo_in ffn_in
            ident_zero ident_ready consts_ready wq_scaled wkk_ready wqk_ready null_q_ready bias_neg
            bias_ready mask_ready ffn_ps0 ffn_ps1 wcat_ready vcat_ps vcat_ready null_ctx_ready
            stats_done mv_done var_done rstd_done xn_done xnt_ps xnt_dve xnt_act k_ps kt_done v_ps v_done
            q_ps q_act q_dve s_ps scores_done exp_done t_ps probs_t_done pv_done
            delta_done p0_done den_done rden_done p0n_done null_part_done attn_mul_done attn_done
            attn_t_ps attn_t_done o_ps ostat_done omv_done ovar_done orstd_done xt_done xtt_ps xtt_done
            f_ps gmax_done gexp_done grec_done gate_done tg_done tgt_ps tgt_done y_ps y_done rest_done
            stored rest_stored wait_taken flag_max flag_ready""".split()
        s = {n: sem(n) for n in NAMES}

        def at(r, per, n):
            return r * per + n

        def held(eng, r):
            if not isinstance(r, int):
                eng.sem_inc(s["wait_taken"], 1)

        def q_of(p):
            return q_late if p else q_all

        def kt_of(p):
            return kt_late if p else kt_all

        block = ctx.enter_context(nc.Block())

        def sp_setup(eng):
            eng.dma_start(x_all[:, :, QT - 1, :],
                          x_d[:, (QT - 1) * P:, :].rearrange("b p d -> p b d")).then_inc(s["x_late_in"], 16)
            eng.dma_start(wkv_raw, wkv_d.rearrange("(c p) n -> p c n", c=DC)).then_inc(s["wkv_in"], 16)
            eng.dma_start(wq[:, :, :], wq_d.rearrange("(c p) n -> p c n", c=DC)).then_inc(s["wq_in"], 16)
            eng.dma_start(bias_late, bias_d[:, (QT - 1) * P:, (QT - 1) * P:]
                          .rearrange("h p k -> p h k")).then_inc(s["bias_in"], 16)
            for b in range(B):
                eng.dma_start(x_all[:, b, 0:QT - 1, :],
                              x_d[b, 0:(QT - 1) * P, :].rearrange("(t p) d -> p t d", p=P)).then_inc(s["x_rest_in"], 16)

        def act_setup_dma(eng):
            with nc.allow_non_contiguous_dma("gains and the null value, one word a partition"):
                eng.dma_start(g_in[:, :], g_in_d.rearrange("(c p) -> p c", c=DC)).then_inc(s["small_in"], 16)
                eng.dma_start(g_out[:, :], g_out_d.rearrange("(c p) -> p c", c=DC)).then_inc(s["small_in"], 16)
                for e in range(2):
                    eng.dma_start(null_vt[e * DH:(e + 1) * DH, :], cond_d[1:2, :].rearrange("a p -> p a")).then_inc(s["small_in"], 16)
            eng.dma_start(null_k[:, :], cond_d[0:1, :].to_broadcast((P, DH))).then_inc(s["small_in"], 16)
            eng.dma_start(null_v[:, :], cond_d[1:2, :].to_broadcast((P, DH))).then_inc(s["small_in"], 16)
            eng.dma_start(null_bias[:, :], nb_d.rearrange("(a h) -> a h", a=1).to_broadcast((P, H))).then_inc(s["small_in"], 16)
            eng.dma_start(mask_raw.rearrange("p b n -> p (b n)"),
                          mask_d.rearrange("(a b) n -> a (b n)", a=1).to_broadcast((P, B * N))).then_inc(s["mask_in"], 16)
            eng.dma_start(w_raw, w_d.rearrange("(o p) d -> p o d", p=P)).then_inc(s["ffn_in"], 16)
            eng.dma_start(u_raw, u_d.rearrange("e r d -> (e r) d")).then_inc(s["ffn_in"], 16)
            eng.dma_start(gate_raw[0:E, :], gate_d).then_inc(s["ffn_in"], 16)
            for c in range(2):
                eng.dma_start(v_raw[:, c, :].rearrange("p (e r) -> p e r", e=E),
                              v_d[:, c * P:(c + 1) * P, :].rearrange("e p r -> p e r")).then_inc(s["ffn_in"], 16)
            eng.dma_start(wo[:, :, :], wo_d.rearrange("(m p) n -> p m n", m=MC)).then_inc(s["wo_in"], 16)

        SMALL = 7 * 16

        def pool_setup(eng):
            g = nc.gpsimd
            g.memset(ident[:, :], 0.0).then_inc(s["ident_zero"], 1)
            eng.wait_ge(s["ident_zero"], 1)
            g.affine_select(out=ident[:, :], in_=ident[:, :], compare_op=ALU.not_equal, fill=1.0, base=0,
                            pattern=[[-1, P]], channel_multiplier=1).then_inc(s["ident_ready"], 1)
            g.memset(pick[:, :], 0.0)
            g.memset(half[:, :], -0.5)
            g.memset(kt_all[:, :, :], 0.0)
            g.memset(kt_late, 0.0).then_inc(s["consts_ready"], 1)
            eng.wait_ge(s["consts_ready"], 1)
            g.memset(pick[0:1, :], 1.0).then_inc(s["consts_ready"], 1)
            eng.wait_ge(s["small_in"], SMALL)
            for c in range(DC):
                eng.wait_ge(s["wq_scaled"], c + 1)
                g.tensor_tensor(wqk[:, c, :, :], wq[:, c, :].rearrange("p (h e) -> p h e", h=H),
                                null_k[:, None, :].to_broadcast((P, H, DH)), ALU.mult).then_inc(s["wqk_ready"], 1)
            eng.wait_ge(s["bias_neg"], 1)
            g.affine_select(out=bias_late, in_=bias_late, compare_op=ALU.is_ge, fill=FAR, base=0,
                            pattern=[[0, H], [-1, P]], channel_multiplier=1).then_inc(s["bias_ready"], 1)

        def pool_general_bias(eng):
            for j in range(QT):
                eng.wait_ge(s["bias_neg"], 2 + j)
                own = bias_all[j][:, :, j * P:(j + 1) * P]
                nc.gpsimd.affine_select(out=own, in_=own, compare_op=ALU.is_ge, fill=FAR, base=0,
                                        pattern=[[0, H], [-1, P]], channel_multiplier=1).then_inc(s["bias_ready"], 1)

        def pool_round(eng, L, r):
            g = nc.gpsimd
            for p in range(L.preps):
                eng.wait_ge(s["var_done"], at(r, L.preps, p + 1))
                g.tensor_tensor(rstd[:, :], mv[:, :, 1], half[:, :], ALU.pow).then_inc(s["rstd_done"], 1)
            for n in range(L.steps):
                for name, t, hf in L.side.get(n, ()):
                    i = 2 * t + hf
                    if name == "den":
                        eng.wait_ge(s["p0n_done"], at(r, 2 * L.tiles, i + 1))
                        g.tensor_tensor(null_part[:, hf, :].rearrange("p (h e) -> p h e", h=8),
                                        small[:, 3, hf, :].unsqueeze(2).to_broadcast((P, 8, DH)),
                                        null_v[:, None, :].to_broadcast((P, 8, DH)), ALU.mult).then_inc(s["null_part_done"], 1)
                    if name == "ctx":
                        eng.wait_ge(s["null_part_done"], at(r, 2 * L.tiles, i + 1))
                        eng.wait_ge(s["attn_mul_done"], at(r, 2 * L.tiles, i + 1))
                        g.tensor_tensor(attn[:, hf, :], attn[:, hf, :], null_part[:, hf, :], ALU.add).then_inc(s["attn_done"], 1)
                    if name == "out":
                        k = t + L.first_side
                        eng.wait_ge(s["ovar_done"], at(r, L.sides, k + 1))
                        g.tensor_tensor(orstd[:, :], omv[:, 1:2], half[:, 0:1], ALU.pow).then_inc(s["orstd_done"], 1)
                    if name == "store" and t < 0:
                        eng.wait_ge(s["y_done"], 1)
                        eng.wait_ge(s["x_rest_in"], 16 * B)
                        for b in range(B):
                            part = x_all[:, b, 0:QT - 1, :]
                            g.tensor_tensor(part, part, y_null[:, None, :].to_broadcast((P, QT - 1, D)),
                                            ALU.add).then_inc(s["rest_done"], 1)

        def dve_setup(eng):
            v = nc.vector
            eng.wait_ge(s["small_in"], SMALL)
            eng.wait_ge(s["wkv_in"], 16)
            for c in range(DC):
                v.tensor_scalar(wkk[:, c, 0:DH], wkv_raw[:, c, 0:DH], g_in[:, c:c + 1], None, ALU.mult)
                v.tensor_scalar(wkk[:, c, DH:P], wkv_raw[:, c, 0:DH], g_in[:, c:c + 1], None, ALU.mult)
                last = v.tensor_scalar(wvn[:, c, 0:DH], wkv_raw[:, c, DH:P], g_in[:, c:c + 1], None, ALU.mult)
            last.then_inc(s["wkk_ready"], 1)
            eng.wait_ge(s["wq_in"], 16)
            for c in range(DC):
                v.tensor_scalar(wq[:, c, :], wq[:, c, :], g_in[:, c:c + 1], -SCALE, ALU.mult, ALU.mult).then_inc(s["wq_scaled"], 1)
            v.tensor_copy(null_ctx[:, :], null_vt[:, 0:1].to_broadcast((P, P))).then_inc(s["null_ctx_ready"], 1)
            eng.wait_ge(s["bias_in"], 16)
            v.tensor_scalar(bias_late, bias_late, -1.0, None, ALU.mult).then_inc(s["bias_neg"], 1)
            eng.wait_ge(s["mask_in"], 16)
            v.tensor_reduce(flag_f[0:1, :], mask_words[0:1, :, 0:(QT - 1) * P // 4], axis=AX.XY, op=ALU.max).then_inc(s["flag_max"], 1)
            eng.wait_ge(s["flag_max"], 1)
            v.tensor_scalar(flag[0:1, :], flag_f[0:1, :], 1.0, None, ALU.min).then_inc(s["flag_ready"], 1)
            v.tensor_scalar(mask_far[:, :, (QT - 1) * P:], mask_raw[:, :, (QT - 1) * P:], -FAR, FAR, ALU.mult, ALU.add).then_inc(s["mask_ready"], 1)
            for c in range(DC):
                eng.wait_ge(s["wqk_ready"], c + 1)
                v.tensor_reduce(wvn[:, c, DH:DH + H], wqk[:, c, :, :], axis=AX.X, op=ALU.add).then_inc(s["null_q_ready"], 1)
            for c, bk in enumerate((x_bank, m_bank)):
                eng.wait_ge(s[f"ffn_ps{c}"], 1)
                v.tensor_scalar(wcat[:, c, :], bk[:, 0:FW], g_out[:, c:c + 1], None, ALU.mult).then_inc(s["wcat_ready"], 1)
            eng.wait_ge(s["vcat_ps"], 1)
            v.tensor_scalar(vcat[:, :], x_bank[:, 0:D], 1.0 / R, None, ALU.mult).then_inc(s["vcat_ready"], 1)

        def dve_general_setup(eng):
            v = nc.vector
            v.tensor_scalar(mask_far[:, :, 0:(QT - 1) * P], mask_raw[:, :, 0:(QT - 1) * P], -FAR, FAR, ALU.mult, ALU.add).then_inc(s["mask_ready"], 1)
            for j in range(QT):
                eng.wait_ge(s[f"bias_in{j}"], 16)
                v.tensor_scalar(bias_all[j], bias_all[j], -1.0, None, ALU.mult).then_inc(s["bias_neg"], 1)

        def dve_round(eng, L, r):
            v = nc.vector
            for p in range(L.preps):
                for j in range(PART):
                    t = PART * p + j
                    xin = x_all[:, t, QT - 1, :] if L.late else x_all[:, r, j, :]
                    if p:
                        eng.wait_ge(s["xn_done"], at(r, L.tiles, PART * p))
                    v.bn_stats(stat[:, j, :], xin).then_inc(s["stats_done"], 1)
                for j in range(PART):
                    eng.wait_ge(s["stats_done"], at(r, L.tiles, PART * p + j + 1))
                    held(eng, r)
                    v.bn_aggr(mv[:, j, :], stat[:, j, :]).then_inc(s["mv_done"], 1)
                eng.wait_ge(s["mv_done"], at(r, L.tiles, PART * p + PART))
                v.tensor_scalar(mv[:, :, 1], mv[:, :, 1], EPS, None, ALU.add).then_inc(s["var_done"], 1)
                eng.wait_ge(s["rstd_done"], at(r, L.preps, p + 1))
                if p:
                    eng.wait_ge(s["xnt_ps"], at(r, 2 * L.preps, 2 * p))
                for j in range(PART):
                    t = PART * p + j
                    xin = x_all[:, t, QT - 1, :] if L.late else x_all[:, r, j, :]
                    v.tensor_scalar(xn[:, j, :], xin, mv[:, j, 0:1], rstd[:, j:j + 1], ALU.subtract, ALU.mult).then_inc(s["xn_done"], 1)
                eng.wait_ge(s["xnt_ps"], at(r, 2 * L.preps, 2 * p + 1))
                v.tensor_copy(xn_t[:, 0, :], t_bank[0][:, :]).then_inc(s["xnt_dve"], 1)
                eng.wait_ge(s["v_ps"], at(r, L.preps, p + 1))
                both = c_bank[1][:, 0:PART * (DH + H)].rearrange("p (j n) -> p j n", j=PART)
                v.tensor_copy(v_all[:, p, :, :], both[:, :, 0:DH])
                v.tensor_tensor(ns_all[:, p, :, :], both[:, :, DH:], null_bias[:, None, :].to_broadcast((P, PART, H)),
                                ALU.subtract).then_inc(s["v_done"], 1)
                for m in range(1, MC, 2):
                    eng.wait_ge(s["q_ps"], at(r, MC * L.preps, MC * p + m + 1))
                    v.tensor_copy(q_of(p)[:, m, :], q_banks[m % 4][:, :]).then_inc(s["q_dve"], 1)

            def scores_of(u):
                t, h0, per = L.units[u]
                nk = L.nk[t]
                eng.wait_ge(s["s_ps"], at(r, L.nu, u + 1))
                if u >= 3:
                    eng.wait_ge(s["exp_done"], at(r, L.nu, u - 2))
                if u == 0:
                    eng.wait_ge(s["v_done"], at(r, L.preps, L.preps))
                    eng.wait_ge(s["bias_ready"], 1 if L.late else 1 + QT)
                held(eng, r)
                for i in range(per):
                    h = h0 + i
                    bias = bias_late[:, h, :] if L.late else bias_all[t][:, h, :]
                    last = v.tensor_tensor_reduce(
                        out=scores[:, u % 3, i * nk:(i + 1) * nk], in0=s_bank[u % 2][:, i * nk:(i + 1) * nk], in1=bias,
                        scale=1.0, scalar=ns_all[:, t // PART, t % PART, h:h + 1], op0=ALU.add, op1=ALU.min,
                        accum_out=neg_max[:, t % 2, h:h + 1])
                last.then_inc(s["scores_done"], 1)

            def probs_t_of(u):
                t, _, per = L.units[u]
                w = per * L.nk[t]
                eng.wait_ge(s["t_ps"], at(r, L.nu, u + 1))
                if u >= 2:
                    eng.wait_ge(s["pv_done"], at(r, L.nu, u - 1))
                v.tensor_copy(probs_t[:, u % 2, 0:w], t_bank[u % 2][:, 0:w]).then_inc(s["probs_t_done"], 1)

            last_unit = {(t, h // 8): u for u, (t, h, _) in enumerate(L.units)}
            for n in range(L.steps):
                if n < L.nu:
                    scores_of(n)
                if 2 <= n < L.nu + 2:
                    probs_t_of(n - 2)
                for name, t, hf in L.side.get(n, ()):
                    i, k = 2 * t + hf, t + L.first_side
                    hs = slice(8 * hf, 8 * hf + 8)
                    if name == "den":
                        eng.wait_ge(s["scores_done"], at(r, L.nu, last_unit[t, hf] + 1))
                        v.tensor_tensor(small[:, 0, hf, :], neg_max[:, t % 2, hs], ns_all[:, t // PART, t % PART, hs],
                                        ALU.subtract).then_inc(s["delta_done"], 1)
                        eng.wait_ge(s["p0_done"], at(r, 2 * L.tiles, i + 1))
                        eng.wait_ge(s["exp_done"], at(r, L.nu, last_unit[t, hf] + 1))
                        v.tensor_tensor(small[:, 2, hf, :], small[:, 1, hf, :], sums[:, t % 2, hs], ALU.add).then_inc(s["den_done"], 1)
                        eng.wait_ge(s["den_done"], at(r, 2 * L.tiles, i + 1))
                        v.reciprocal(small[:, 4, hf, :], small[:, 2, hf, :]).then_inc(s["rden_done"], 1)
                        eng.wait_ge(s["rden_done"], at(r, 2 * L.tiles, i + 1))
                        v.tensor_tensor(small[:, 3, hf, :], small[:, 1, hf, :], small[:, 4, hf, :], ALU.mult).then_inc(s["p0n_done"], 1)
                    if name == "ctx":
                        eng.wait_ge(s["pv_done"], at(r, L.nu, last_unit[t, hf] + 1))
                        if t:
                            eng.wait_ge(s["attn_t_ps"], at(r, 2 * L.tiles, i - 1))
                        v.tensor_tensor(attn[:, hf, :].rearrange("p (h e) -> p h e", h=8),
                                        c_bank[hf][:, :].rearrange("p (h e) -> p h e", h=8),
                                        small[:, 4, hf, :].unsqueeze(2).to_broadcast((P, 8, DH)), ALU.mult).then_inc(s["attn_mul_done"], 1)
                    if name == "out":
                        eng.wait_ge(s["o_ps"], at(r, L.sides, k + 1))
                        v.bn_stats(ostat[:, :], m_bank[:, 0:D]).then_inc(s["ostat_done"], 1)
                        eng.wait_ge(s["ostat_done"], at(r, L.sides, k + 1))
                        held(eng, r)
                        v.bn_aggr(omv[:, :], ostat[:, :]).then_inc(s["omv_done"], 1)
                        eng.wait_ge(s["omv_done"], at(r, L.sides, k + 1))
                        v.tensor_scalar(omv[:, 1:2], omv[:, 1:2], EPS, None, ALU.add).then_inc(s["ovar_done"], 1)
                    if name == "norm":
                        eng.wait_ge(s["orstd_done"], at(r, L.sides, k + 1))
                        v.tensor_scalar(xt[:, :], m_bank[:, 0:D], omv[:, 0:1], orstd[:, 0:1],
                                        ALU.subtract, ALU.mult).then_inc(s["xt_done"], 1)
                    if name == "gate":
                        eng.wait_ge(s["f_ps"], at(r, L.sides, k + 1))
                        v.tensor_reduce(gate_s[:, 0, 0:1], m_bank[:, D + E * R:FW], axis=AX.X, op=ALU.max,
                                        negate=True).then_inc(s["gmax_done"], 1)
                        eng.wait_ge(s["gexp_done"], at(r, L.sides, k + 1))
                        v.reciprocal(gate_s[:, 0, 2:3], gate_s[:, 0, 1:2]).then_inc(s["grec_done"], 1)
                        eng.wait_ge(s["grec_done"], at(r, L.sides, k + 1))
                        v.tensor_scalar(gate_s[:, 2, :], gate_s[:, 1, :], gate_s[:, 0, 2:3], None, ALU.mult).then_inc(s["gate_done"], 1)
                        eng.wait_ge(s["gate_done"], at(r, L.sides, k + 1))
                        v.tensor_tensor(tg[:, :].rearrange("p (e q) -> p e q", e=E),
                                        m_bank[:, D:D + E * R].rearrange("p (e q) -> p e q", e=E),
                                        gate_s[:, 2, :].unsqueeze(2).to_broadcast((P, E, R)), ALU.mult).then_inc(s["tg_done"], 1)
                    if name == "store":
                        eng.wait_ge(s["y_ps"], at(r, L.sides, k + 1))
                        if t < 0:
                            v.tensor_copy(y_null[:, :], m_bank[:, 0:D]).then_inc(s["y_done"], 1)
                        else:
                            row = x_all[:, t, QT - 1, :] if L.late else x_all[:, r, t, :]
                            v.tensor_tensor(row, m_bank[:, 0:D], row, ALU.add).then_inc(s["y_done"], 1)

        def act_round(eng, L, r):
            a = nc.scalar
            for p in range(L.preps):
                eng.wait_ge(s["xnt_ps"], at(r, 2 * L.preps, 2 * p + 2))
                a.activation(xn_t[:, 1, :], t_bank[1][:, :], ACT.Copy).then_inc(s["xnt_act"], 1)
                eng.wait_ge(s["k_ps"], at(r, L.preps, p + 1))
                a.activation(kt_of(p)[0:DH, 0, :], c_bank[0][0:DH, :], ACT.Copy)
                a.activation(kt_of(p)[DH:P, 1, :], c_bank[0][DH:P, :], ACT.Copy).then_inc(s["kt_done"], 1)
                for m in range(0, MC, 2):
                    eng.wait_ge(s["q_ps"], at(r, MC * L.preps, MC * p + m + 1))
                    a.activation(q_of(p)[:, m, :], q_banks[m % 4][:, :], ACT.Copy).then_inc(s["q_act"], 1)

            for n in range(L.steps):
                if n < L.nu:
                    t, h0, per = L.units[n]
                    nk = L.nk[t]
                    eng.wait_ge(s["scores_done"], at(r, L.nu, n + 1))
                    if n >= 3:
                        eng.wait_ge(s["t_ps"], at(r, L.nu, n - 2))
                    for i in range(per):
                        h = h0 + i
                        last = a.activation(probs[:, n % 3, i * nk:(i + 1) * nk], scores[:, n % 3, i * nk:(i + 1) * nk],
                                            ACT.Exp, bias=neg_max[:, t % 2, h:h + 1], scale=-1.0,
                                            accum_out=sums[:, t % 2, h:h + 1])
                    last.then_inc(s["exp_done"], 1)
                for name, t, hf in L.side.get(n, ()):
                    i, k = 2 * t + hf, t + L.first_side
                    if name == "den":
                        eng.wait_ge(s["delta_done"], at(r, 2 * L.tiles, i + 1))
                        a.activation(small[:, 1, hf, :], small[:, 0, hf, :], ACT.Exp).then_inc(s["p0_done"], 1)
                    if name == "turn":
                        eng.wait_ge(s["attn_t_ps"], at(r, 2 * L.tiles, i + 1))
                        a.activation(attn_t[:, 4 * hf:4 * hf + 4, :], x_bank[:, :].rearrange("p (m q) -> p m q", m=4),
                                     ACT.Copy).then_inc(s["attn_t_done"], 1)
                    if name == "norm":
                        eng.wait_ge(s["xtt_ps"], at(r, L.sides, k + 1))
                        a.activation(xt_t[:, :, :], x_bank[:, 0:D].rearrange("p (c q) -> p c q", c=DC), ACT.Copy).then_inc(s["xtt_done"], 1)
                    if name == "gate":
                        eng.wait_ge(s["gmax_done"], at(r, L.sides, k + 1))
                        a.activation(gate_s[:, 1, :], m_bank[:, D + E * R:FW], ACT.Exp, bias=gate_s[:, 0, 0:1],
                                     accum_out=gate_s[:, 0, 1:2]).then_inc(s["gexp_done"], 1)
                    if name == "lora":
                        eng.wait_ge(s["tgt_ps"], at(r, L.sides, k + 1))
                        a.activation(tg_t[:, :], x_bank[:, 0:P], ACT.Copy).then_inc(s["tgt_done"], 1)

        def pe_setup(eng):
            pe = nc.tensor
            eng.wait_ge(s["ident_ready"], 1)
            eng.wait_ge(s["ffn_in"], 16 * 5)
            for c, bk in enumerate((x_bank, m_bank)):
                cols = slice(c * P, (c + 1) * P)
                for o2 in range(2):
                    pe.transpose(bk[:, o2 * P:(o2 + 1) * P], w_raw[:, o2, cols], ident[:, :])
                pe.transpose(bk[:, D:D + P], u_raw[:, cols], ident[:, :])
                pe.transpose(bk[:, D + P:FW], gate_raw[0:E, cols], ident[0:E, 0:E]).then_inc(s[f"ffn_ps{c}"], 1)
            eng.wait_ge(s["wcat_ready"], 1)
            pe.transpose(x_bank[:, 0:P], v_raw[:, 0, :], ident[:, :])
            pe.transpose(x_bank[:, P:D], v_raw[:, 1, :], ident[:, :]).then_inc(s["vcat_ps"], 1)

        def pe_round(eng, L, r, first):
            pe = nc.tensor
            for p in range(L.preps):
                for c in range(DC):
                    if c == 0 and p:
                        eng.wait_ge(s["q_act"], at(r, 4 * L.preps, 4 * p))
                        eng.wait_ge(s["q_dve"], at(r, 4 * L.preps, 4 * p))
                    for j in range(PART):
                        if c == 0:
                            eng.wait_ge(s["xn_done"], at(r, L.tiles, PART * p + j + 1))
                        last = pe.transpose(t_bank[c][:, j * P:(j + 1) * P], xn[:, j, c * P:(c + 1) * P], ident[:, :])
                    last.then_inc(s["xnt_ps"], 1)
                eng.wait_ge(s["xnt_dve"], at(r, L.preps, p + 1))
                eng.wait_ge(s["xnt_act"], at(r, L.preps, p + 1))
                if first and p == 0:
                    eng.wait_ge(s["wkk_ready"], 1)
                for c in range(DC):
                    last = pe.matmul(c_bank[0][:, :], wkk[:, c, :], xn_t[:, c, :], start=(c == 0), stop=(c == DC - 1))
                last.then_inc(s["k_ps"], 1)
                if first and p == 0:
                    eng.wait_ge(s["null_q_ready"], DC)
                if p:
                    eng.wait_ge(s["v_done"], at(r, L.preps, p))
                for j in range(PART):
                    for c in range(DC):
                        last = pe.matmul(c_bank[1][:, j * (DH + H):(j + 1) * (DH + H)], xn_t[:, c, j * P:(j + 1) * P],
                                         wvn[:, c, :], start=(c == 0), stop=(c == DC - 1))
                last.then_inc(s["v_ps"], 1)
                for m in range(MC):
                    if m >= 4:
                        eng.wait_ge(s["q_dve" if m % 2 else "q_act"], at(r, 4 * L.preps, 4 * p + m // 2 - 1))
                    for c in range(DC):
                        last = pe.matmul(q_banks[m % 4][:, :], wq[:, c, m * P:(m + 1) * P], xn_t[:, c, :],
                                         start=(c == 0), stop=(c == DC - 1))
                    last.then_inc(s["q_ps"], 1)
            eng.wait_ge(s["q_act"], at(r, 4 * L.preps, 4 * L.preps))
            eng.wait_ge(s["q_dve"], at(r, 4 * L.preps, 4 * L.preps))
            eng.wait_ge(s["kt_done"], at(r, L.preps, L.preps))
            eng.wait_ge(s["v_done"], at(r, L.preps, L.preps))
            if first:
                eng.wait_ge(s["mask_ready"], 1 if L.late else 2)
                eng.wait_ge(s["consts_ready"], 2)
                eng.wait_ge(s["null_ctx_ready"], 1)
                eng.wait_ge(s["vcat_ready"], 1)
                eng.wait_ge(s["wcat_ready"], 2)
                eng.wait_ge(s["wo_in"], 16)

            last_unit = {(t, h // 8): u for u, (t, h, _) in enumerate(L.units)}
            for n in range(L.steps):
                if n < L.nu:
                    t, h0, per = L.units[n]
                    nk, k0, p, j = L.nk[t], L.k0[t], t // PART, t % PART
                    bk = s_bank[n % 2]
                    if n >= 2:
                        eng.wait_ge(s["scores_done"], at(r, L.nu, n - 1))
                    if L.late:
                        far = mask_far[:, t, (QT - 1) * P:]
                    else:
                        far = mask_far[:, r, 0:nk]
                    pe.matmul(bk[:, 0:per * nk], pick[:, :], far.unsqueeze(1).to_broadcast((P, per, nk)), start=True, stop=False)
                    if per == 1:
                        last = pe.matmul(bk[:, 0:nk], q_of(p)[:, h0 // 2, j * P:(j + 1) * P],
                                         kt_of(p)[:, h0 % 2, k0:k0 + nk], start=False, stop=True)
                    else:
                        for i in range(0, per, 2):
                            last = pe.matmul(bk[:, i * nk:(i + 2) * nk].rearrange("p (e k) -> p e k", e=2),
                                             q_of(p)[:, (h0 + i) // 2, j * P:(j + 1) * P],
                                             kt_of(p)[:, :, k0:k0 + nk], start=False, stop=(i == per - 2))
                    last.then_inc(s["s_ps"], 1)
                if 2 <= n < L.nu + 2:
                    u = n - 2
                    t, h0, per = L.units[u]
                    eng.wait_ge(s["exp_done"], at(r, L.nu, u + 1))
                    if u >= 2:
                        eng.wait_ge(s["probs_t_done"], at(r, L.nu, u - 1))
                    for i in range(per * L.nk[t] // P):
                        last = pe.transpose(t_bank[u % 2][:, i * P:(i + 1) * P], probs[:, u % 3, i * P:(i + 1) * P], ident[:, :])
                    last.then_inc(s["t_ps"], 1)
                if 3 <= n < L.nu + 3:
                    u = n - 3
                    t, h0, per = L.units[u]
                    nb = L.nk[t] // P
                    eng.wait_ge(s["probs_t_done"], at(r, L.nu, u + 1))
                    if h0 % 8 == 0 and t:
                        eng.wait_ge(s["attn_mul_done"], at(r, 2 * L.tiles, 2 * (t - 1) + h0 // 8 + 1))
                    for i in range(per):
                        h = h0 + i
                        for kb in range(nb):
                            last = pe.matmul(c_bank[h // 8][:, (h % 8) * DH:(h % 8 + 1) * DH],
                                             probs_t[:, u % 2, (i * nb + kb) * P:(i * nb + kb + 1) * P],
                                             v_all[:, t // PART, L.k0[t] // P + kb, :], start=(kb == 0), stop=(kb == nb - 1))
                    last.then_inc(s["pv_done"], 1)
                for name, t, hf in L.side.get(n, ()):
                    i, k = 2 * t + hf, t + L.first_side
                    if name == "turn":
                        eng.wait_ge(s["attn_done"], at(r, 2 * L.tiles, i + 1))
                        if i:
                            eng.wait_ge(s["attn_t_done"], at(r, 2 * L.tiles, i))
                        if k:
                            eng.wait_ge(s["xtt_done"], at(r, L.sides, x_reads(L, n, t, hf)[0]))
                            eng.wait_ge(s["tgt_done"], at(r, L.sides, x_reads(L, n, t, hf)[1]))
                        for m in range(4):
                            last = pe.transpose(x_bank[:, m * P:(m + 1) * P], attn[:, hf, m * P:(m + 1) * P], ident[:, :])
                        last.then_inc(s["attn_t_ps"], 1)
                    if name == "out":
                        if t >= 0:
                            eng.wait_ge(s["attn_t_done"], at(r, 2 * L.tiles, 2 * t + 2))
                        if k:
                            eng.wait_ge(s["y_done"], at(r, L.sides, k))
                        for m in range(MC):
                            last = pe.matmul(m_bank[:, 0:D], null_ctx[:, :] if t < 0 else attn_t[:, m, :], wo[:, m, :],
                                             start=(m == 0), stop=(m == MC - 1))
                        last.then_inc(s["o_ps"], 1)
                    if name == "norm":
                        eng.wait_ge(s["xt_done"], at(r, L.sides, k + 1))
                        free_x(eng, L, r, n, name, t, hf)
                        for c in range(DC):
                            last = pe.transpose(x_bank[:, c * P:(c + 1) * P], xt[:, c * P:(c + 1) * P], ident[:, :])
                        last.then_inc(s["xtt_ps"], 1)
                    if name == "ffn":
                        eng.wait_ge(s["xtt_done"], at(r, L.sides, k + 1))
                        for c in range(DC):
                            last = pe.matmul(m_bank[:, 0:FW], xt_t[:, c, :], wcat[:, c, :], start=(c == 0), stop=(c == DC - 1))
                        last.then_inc(s["f_ps"], 1)
                    if name == "lora":
                        eng.wait_ge(s["tg_done"], at(r, L.sides, k + 1))
                        free_x(eng, L, r, n, name, t, hf)
                        pe.transpose(x_bank[:, 0:P], tg[:, :], ident[:, :]).then_inc(s["tgt_ps"], 1)
                        eng.wait_ge(s["tgt_done"], at(r, L.sides, k + 1))
                        pe.matmul(m_bank[:, 0:D], tg_t[:, :], vcat[:, :], start=False, stop=True,
                                  skip_group_check=True).then_inc(s["y_ps"], 1)

        def uses_of_x(L, n, piece):
            seen = {"turn": 0, "norm": 0, "lora": 0}
            for m in range(n + 1):
                for q in L.side.get(m, ()):
                    if m == n and q == piece:
                        return seen
                    if q[0] in seen:
                        seen[q[0]] += 1
            return seen

        def free_x(eng, L, r, n, name, t, hf):
            seen = uses_of_x(L, n, (name, t, hf))
            if seen["turn"]:
                eng.wait_ge(s["attn_t_done"], at(r, 2 * L.tiles, seen["turn"]))
            if seen["norm"]:
                eng.wait_ge(s["xtt_done"], at(r, L.sides, seen["norm"]))
            if seen["lora"]:
                eng.wait_ge(s["tgt_done"], at(r, L.sides, seen["lora"]))

        def x_reads(L, n, t, hf):
            seen = uses_of_x(L, n, ("turn", t, hf))
            return seen["norm"], seen["lora"]

        LATE, ALL = Layout(True), Layout(False)

        def act_late_store(eng):
            for b in range(B):
                eng.wait_ge(s["rest_done"], b + 1)
                eng.dma_start(out_d[b, 0:(QT - 1) * P, :].rearrange("(t p) d -> p t d", p=P),
                              x_all[:, b, 0:QT - 1, :]).then_inc(s["rest_stored"], 16)
            eng.wait_ge(s["rest_stored"], 16 * B)

        def sp_general_bias(eng):
            eng.wait_ge(s["bias_ready"], 1)
            eng.wait_ge(s["vcat_ready"], 1)
            eng.wait_ge(s["null_q_ready"], DC)
            eng.wait_ge(s["mask_ready"], 2)
            eng.wait_ge(s["consts_ready"], 2)
            for j in range(QT):
                eng.dma_start(bias_all[j], bias_d[:, j * P:(j + 1) * P, 0:(j + 1) * P]
                              .rearrange("h p k -> p h k")).then_inc(s[f"bias_in{j}"], 16)

        def sp_round(eng, L, r):
            for t in range(-L.first_side, L.tiles):
                if t < 0:
                    continue
                eng.wait_ge(s["y_done"], at(r, L.sides, t + L.first_side + 1))
                if L.late:
                    eng.dma_start(out_d[t, (QT - 1) * P:, :], x_all[:, t, QT - 1, :]).then_inc(s["stored"], 16)
                else:
                    eng.dma_start(out_d[r, t * P:(t + 1) * P, :] if isinstance(r, int) else
                                  out_d[bass.ds(r, 1), t * P:(t + 1) * P, :].rearrange("a p d -> (a p) d"),
                                  x_all[:, r, t, :]).then_inc(s["stored"], 16)

        def paths(eng, late, general, body, finish=lambda L: None):
            eng.wait_ge(s["flag_ready"], 1)
            early = eng.value_load(flag[0:1, 0:1], min_val=0, max_val=1)
            with eng.If(early == 0):
                body(LATE, 0, True)
                late()
                finish(LATE)
            with eng.Else():
                general()
                body(ALL, 0, True)
                with eng.Fori(1, B) as r:
                    body(ALL, r, False)
                finish(ALL)

        def nothing():
            pass

        @block.sync
        def _(sp):
            sp_setup(sp)
            paths(sp, nothing, lambda: sp_general_bias(sp), lambda L, r, first: sp_round(sp, L, r),
                  lambda L: sp.wait_ge(s["stored"], 16 * (B if L.late else B * QT)))

        @block.gpsimd
        def _(pool):
            pool_setup(pool)
            paths(pool, nothing, lambda: pool_general_bias(pool), lambda L, r, first: pool_round(pool, L, r))

        @block.scalar
        def _(act):
            act_setup_dma(act)
            paths(act, lambda: act_late_store(act), nothing, lambda L, r, first: act_round(act, L, r))

        @block.vector
        def _(dve):
            dve_setup(dve)
            dve.wait_ge(s["x_late_in"], 16)
            paths(dve, nothing, lambda: dve_general_setup(dve), lambda L, r, first: dve_round(dve, L, r))

        @block.tensor
        def _(pe):
            pe_setup(pe)
            paths(pe, nothing, nothing, lambda L, r, first: pe_round(pe, L, r, first))


_INS = ["x", "fside_16xSxS_0", "cond_64", "mask_BxS_bk0", "L0_cond_g_in", "L0_cond_null_attn_bias", "L0_cond_Wq",
        "L0_cond_Wkv", "L0_cond_Wo", "L0_cond_g_out", "L0_ffn_weight", "L0_ffn_gate_w", "L0_ffn_lora_U",
        "L0_ffn_lora_V"]


def kernel(**inputs):
    import numpy as np
    import concourse.bacc as bacc
    from concourse import mybir as mb
    from concourse.bass_utils import run_bass_kernel_spmd

    nc = bacc.Bacc("TRN2", target_bir_lowering=False, num_devices=1)
    arrays, args = {}, []
    for name in _INS:
        a = np.ascontiguousarray(inputs[name])
        arrays[f"in_{name}"] = a
        args.append(nc.dram_tensor(f"in_{name}", a.shape, mb.dt.from_np(a.dtype), kind="ExternalInput").ap())
    args.append(nc.dram_tensor("out", (B, N, D), mb.dt.float32, kind="ExternalOutput").ap())
    attention_ffn(nc, *args)
    r = run_bass_kernel_spmd(nc, [arrays], core_ids=[0])
    return r.results[0]["out"]
```

```python
from contextlib import ExitStack

import concourse.bass as bass
from concourse import mybir

ALU = mybir.AluOpType
ACT = mybir.ActivationFunctionType
AX = mybir.AxisListType
F32 = mybir.dt.float32
BF16 = mybir.dt.bfloat16
U8 = mybir.dt.uint8
I32 = mybir.dt.int32

P = 128
B, N, D = 8, 512, 256
H, DH = 16, 64
INNER = H * DH
DC = D // P
MC = INNER // P
QT = N // P
E, R = 8, 16
EPS = 1e-5
SCALE = DH ** -0.5
FAR = 1e30
FW = D + E * R + E
PART = 4
WARM = 16


class Layout:

    def __init__(self, late):
        self.late = late
        self.rounds = 1 if late else B
        self.preps = 2 if late else 1
        self.tiles = PART * self.preps
        self.nk = [P if late else P * (t + 1) for t in range(self.tiles)]
        self.k0 = [P * (t % PART) if late else 0 for t in range(self.tiles)]
        self.units = []
        for t in range(self.tiles):
            per = {P: 4, 2 * P: 2}.get(self.nk[t], 1)
            self.units += [(t, h, per) for h in range(0, H, per)]
        self.nu = len(self.units)
        self.first_side = 1 if late else 0
        self.sides = self.tiles + self.first_side
        self.batches = [[-1], [0, 1, 2, 3], [4, 5], [6, 7]] if late else [[0, 1, 2, 3]]
        self.last_unit = {(t, h // 8): u for u, (t, h, _) in enumerate(self.units)}
        self.side = {}
        u1 = {-1: -7, **{t: self.last_unit[t, 1] for t in range(self.tiles)}}
        for t in range(self.tiles):
            for hf in range(2):
                self.put(self.last_unit[t, hf], HALF_STAGES, t, hf)
        for t in range(-self.first_side, self.tiles):
            self.put(u1[t], TILE_STAGES, t, 0)
        self.pairs = []
        for k, batch in enumerate(self.batches):
            self.put(u1[batch[-1]], BATCH_STAGES, batch[-1], k)
            for m in range(0, len(batch), 2):
                self.put(u1[batch[-1]] + 2 * m, PAIR_STAGES, batch[-1], len(self.pairs))
                self.pairs.append((k, batch[m:m + 2]))
        self.steps = max(self.side) + 1
        self.order = [(n, x) for n in range(self.steps) for x in self.side.get(n, ())]
        self.x_uses = [x for _, x in self.order if x[0] in ("turn", "xtt", "tgt")]
        self.f_uses = [x for _, x in self.order if x[0] in ("ffn", "lora")]

    def put(self, start, stages, t, k):
        for lag, name in stages:
            pieces = self.side.setdefault(start + lag, [])
            pieces.append((name, t, k))
            pieces.sort(key=lambda x: (x[1], STAGE_ORDER.index(x[0]), x[2]))

    def at(self, n):
        return self.side.get(n, ())


HALF_STAGES = ((0, "delta"), (1, "p0"), (2, "den"), (4, "ctx"), (6, "turn"))
TILE_STAGES = ((7, "out"), (8, "out_end"), (9, "stat"), (10, "norm"), (11, "xtt"), (12, "ffn"), (13, "base"))
BATCH_STAGES = ((14, "gmax"), (15, "gexp"), (16, "gate"), (17, "tgt"))
PAIR_STAGES = ((18, "lora"), (19, "fin"))
STAGE_ORDER = [name for stages in (HALF_STAGES, TILE_STAGES, BATCH_STAGES, PAIR_STAGES) for _, name in stages]


def attention_ffn(nc, x_d, bias_d, cond_d, mask_d, g_in_d, nb_d, wq_d, wkv_d, wo_d, g_out_d,
                  w_d, gate_d, u_d, v_d, out_d):
    ctx = ExitStack()
    with ctx:
        def sb(name, shape, dt=F32):
            return ctx.enter_context(nc.sbuf_tensor(name, shape, dt))

        def bank(name):
            return ctx.enter_context(nc.psum_tensor(name, [P, 512], F32))

        def sem(name):
            return ctx.enter_context(nc.semaphore(name))

        x_all = sb("x_all", [P, B, QT, D])
        ident = sb("ident", [P, P])
        wq = sb("wq", [P, DC, INNER])
        wkk = sb("wkk", [P, DC, P])
        wvn = sb("wvn", [P, DC, DH + H])
        wo = sb("wo", [P, MC, D])
        wcat = sb("wcat", [P, DC, FW])
        vcat = sb("vcat", [P, D])
        g_in = sb("g_in", [P, DC])
        g_out = sb("g_out", [P, DC])
        null_k = sb("null_k", [P, DH])
        null_v = sb("null_v", [P, DH])
        null_vt = sb("null_vt", [P, 1])
        null_ctx = sb("null_ctx", [P, P])
        null_bias = sb("null_bias", [P, H])
        y_null = sb("y_null", [P, D])
        pick = sb("pick", [P, P], BF16)
        mask_room = sb("mask_room", [P, B * N // 2])
        mask_far = mask_room[:, :].bitcast(BF16).rearrange("p (b n) -> p b n", b=B)
        mask_late = mask_room[:, 0:B * P].rearrange("p (b n) -> p b n", b=B)
        mask_row = sb("mask_row", [1, B, N], U8)
        xn_t = sb("xn_t", [P, DC, N])
        q_all = sb("q_all", [P, MC, N])
        kt_all = sb("kt_all", [P, 2, N])
        v_all = sb("v_all", [P, 2, PART, DH])
        ns_all = sb("ns_all", [P, 2, PART, H])
        probs = sb("probs", [P, 3, 512])
        xn = probs[:, 0:2, :].rearrange("p a (j d) -> p (a j) d", d=D)
        probs_t = sb("probs_t", [P, 2, 512])
        attn = sb("attn", [P, 2, 512])
        null_part = sb("null_part", [P, 2, 512])
        attn_t = sb("attn_t", [P, MC, P])
        xt = sb("xt", [P, D])
        xt_t = sb("xt_t", [P, DC, P])
        tg = sb("tg", [P, PART, E * R])
        tg_t = sb("tg_t", [P, PART, P])
        lora_in = sb("lora_in", [P, PART, FW - D])
        stat = sb("stat", [P, 2 * PART, 6])
        mv = sb("mv", [P, 2 * PART, 2])
        rstd = sb("rstd", [P, 2 * PART])
        half = sb("half", [P, 2 * PART])
        neg_max = sb("neg_max", [P, 2, H])
        sums = sb("sums", [P, 2, H])
        small = sb("small", [P, 5, 2, 8])
        ostat = sb("ostat", [P, 6])
        omv = sb("omv", [P, 2])
        orstd = sb("orstd", [P, 1])
        flag_f = sb("flag_f", [P, 1])
        flag = sb("flag", [P, 1], I32)
        gate_s = sb("gate_s", [P, 2, PART, E])
        gate_1 = sb("gate_1", [P, 3, PART])
        big = sb("big", [P, H * P * (1 + 2 + 3 + 4)])
        starts = [0, H * P, 3 * H * P, 6 * H * P]
        bias_all = [big[:, s:s + H * P * (j + 1)].rearrange("p (h k) -> p h k", h=H)
                    for j, s in enumerate(starts)]
        o = [0]

        def carve(n):
            o[0] += n
            return big[:, o[0] - n:o[0]]

        bias_late = carve(H * P).rearrange("p (h k) -> p h k", h=H)
        q_late = carve(MC * N).rearrange("p (m n) -> p m n", m=MC)
        kt_late = carve(2 * N).rearrange("p (e n) -> p e n", e=2)
        xn_t_late = carve(DC * N).rearrange("p (c n) -> p c n", c=DC)
        wo_sum = carve(D)
        xn_late = carve(PART * D).rearrange("p (j d) -> p j d", j=PART)
        lora_in_late = carve(PART * (FW - D)).rearrange("p (j n) -> p j n", j=PART)
        w_raw = carve(2 * D).rearrange("p (o d) -> p o d", o=2)
        u_raw = carve(D)
        gate_raw = carve(D)
        v_raw = carve(2 * E * R).rearrange("p (o n) -> p o n", o=2)
        wkv_raw = carve(DC * P).rearrange("p (c n) -> p c n", c=DC)
        wqk = carve(DC * INNER).rearrange("p (c h e) -> p c h e", c=DC, h=H)
        mask_late_raw = carve(B * P // 4).bitcast(U8).rearrange("p (b n) -> p b n", b=B)
        bias_masked = carve(2 * H * P).rearrange("p (t h k) -> p t h k", t=2, h=H)

        s_bank = [bank("s_bank0"), bank("s_bank1")]
        t_bank = bank("t_bank")
        c_bank = [bank("c_bank0"), bank("c_bank1")]
        x_bank = bank("x_bank")
        o_bank = bank("o_bank")
        f_bank = bank("f_bank")
        q_banks = s_bank + [t_bank, x_bank]
        xn_banks = [o_bank, f_bank]

        NAMES = """x_late_in0 x_late_in1 x_rest_in wq_in wkv_in small_in mask_in mask_late_in bias_masked_ready mask_zero g_in_in null_k_in bias_in bias_in0 bias_in1 bias_in2 bias_in3 wo_in ffn_in
            ident_zero ident_ready consts_ready wq_scaled wkk_ready wqk_ready null_q_ready bias_neg
            bias_ready mask_ready ffn_ps0 ffn_ps1 wcat_ready vcat_ps vcat_ready null_ctx_ready wo_sum_ready
            stats_done mv_done var_done rstd_done xn_done xnt_ps xnt_dve xnt_act k_ps kt_done v_ps v_done
            q_ps q_act q_dve s_ps scores_done exp_done t_ps probs_t_done pv_done
            delta_done p0_done den_done rden_done p0n_done null_part_done attn_mul_done attn_done
            x_ps x_read o_ps ostat_done omv_done ovar_done orstd_done xt_done
            f_ps f_read lora_in_done gmax_done gsub_done gexp_done gsum_done grec_done gate_done tg_done rest_done
            stored rest_stored wait_taken flag_max flag_ready""".split()
        s = {n: sem(n) for n in NAMES}

        def at(r, per, n):
            return r * per + n

        def held(eng, r):
            if not isinstance(r, int):
                eng.sem_inc(s["wait_taken"], 1)

        def q_of(p):
            return q_late if p else q_all

        def xn_of(L, t):
            return xn_late[:, t - PART, :] if t >= PART else xn[:, t, :]

        def lora_in_of(L, t0, n):
            if t0 >= PART:
                return lora_in_late[:, t0 - PART:t0 - PART + n, :]
            return lora_in[:, max(t0, 0):max(t0, 0) + n, :]

        def x_use(L, piece):
            return L.x_uses.index(piece)

        def f_use(L, piece):
            return L.f_uses.index(piece)

        def xn_t_of(p):
            return xn_t_late if p else xn_t

        def kt_of(p):
            return kt_late if p else kt_all

        block = ctx.enter_context(nc.Block())

        def x_late_load(eng, k):
            eng.dma_start(x_all[:, PART * k:PART * (k + 1), QT - 1, :],
                          x_d[PART * k:PART * (k + 1), (QT - 1) * P:, :].rearrange("b p d -> p b d")).then_inc(s[f"x_late_in{k}"], 16)

        def sp_setup(eng):
            eng.dma_start(mask_row.rearrange("a b n -> a (b n)"),
                          mask_d.rearrange("(a b) n -> a (b n)", a=1)).then_inc(s["mask_in"], 16)
            eng.dma_start(wkv_raw, wkv_d.rearrange("(c p) n -> p c n", c=DC)).then_inc(s["wkv_in"], 16)
            eng.dma_start(wq[:, :, :], wq_d.rearrange("(c p) n -> p c n", c=DC)).then_inc(s["wq_in"], 16)
            x_late_load(eng, 1)
            eng.dma_start(bias_late, bias_d[:, (QT - 1) * P:, (QT - 1) * P:]
                          .rearrange("h p k -> p h k")).then_inc(s["bias_in"], 16)
            eng.dma_start(w_raw, w_d.rearrange("(o p) d -> p o d", p=P)).then_inc(s["ffn_in"], 16)
            eng.dma_start(u_raw, u_d.rearrange("e r d -> (e r) d")).then_inc(s["ffn_in"], 16)
            eng.dma_start(gate_raw[0:E, :], gate_d).then_inc(s["ffn_in"], 16)
            for c in range(2):
                eng.dma_start(v_raw[:, c, :].rearrange("p (e r) -> p e r", e=E),
                              v_d[:, c * P:(c + 1) * P, :].rearrange("e p r -> p e r")).then_inc(s["ffn_in"], 16)
            eng.dma_start(wo[:, :, :], wo_d.rearrange("(m p) n -> p m n", m=MC)).then_inc(s["wo_in"], 16)
            for b in range(B):
                eng.dma_start(x_all[:, b, 0:QT - 1, :],
                              x_d[b, 0:(QT - 1) * P, :].rearrange("(t p) d -> p t d", p=P)).then_inc(s["x_rest_in"], 16)

        def act_setup_dma(eng):
            x_late_load(eng, 0)
            with nc.allow_non_contiguous_dma("gains and the null value, one word a partition"):
                eng.dma_start(g_in[:, :], g_in_d.rearrange("(c p) -> p c", c=DC)).then_inc(s["g_in_in"], 16)
                eng.dma_start(null_k[:, :], cond_d[0:1, :].to_broadcast((P, DH))).then_inc(s["null_k_in"], 16)
                eng.dma_start(mask_late_raw, mask_d[:, (QT - 1) * P:].unsqueeze(0).to_broadcast((P, B, P))).then_inc(s["mask_late_in"], 16)
                eng.dma_start(null_bias[:, :], nb_d.rearrange("(a h) -> a h", a=1).to_broadcast((P, H))).then_inc(s["small_in"], 16)
                eng.dma_start(null_v[:, :], cond_d[1:2, :].to_broadcast((P, DH))).then_inc(s["small_in"], 16)
                for e in range(2):
                    eng.dma_start(null_vt[e * DH:(e + 1) * DH, :], cond_d[1:2, :].rearrange("a p -> p a")).then_inc(s["small_in"], 16)
                eng.dma_start(g_out[:, :], g_out_d.rearrange("(c p) -> p c", c=DC)).then_inc(s["small_in"], 16)

        SMALL = 5 * 16

        def pool_setup(eng):
            g = nc.gpsimd
            g.memset(ident[:, :], 0.0).then_inc(s["ident_zero"], 1)
            eng.wait_ge(s["ident_zero"], 1)
            g.affine_select(out=ident[:, :], in_=ident[:, :], compare_op=ALU.not_equal, fill=1.0, base=0,
                            pattern=[[-1, P]], channel_multiplier=1).then_inc(s["ident_ready"], 1)
            g.memset(pick[:, :], 0.0)
            g.memset(half[:, :], -0.5)
            g.memset(kt_all[:, :, :], 0.0)
            g.memset(kt_late, 0.0).then_inc(s["consts_ready"], 1)
            eng.wait_ge(s["consts_ready"], 1)
            g.memset(pick[0:1, :], 1.0).then_inc(s["consts_ready"], 1)

        def pool_null_key(eng):
            g = nc.gpsimd
            eng.wait_ge(s["null_k_in"], 16)
            for c in range(DC):
                eng.wait_ge(s["wq_scaled"], c + 1)
                g.tensor_tensor(wqk[:, c, :, :], wq[:, c, :].rearrange("p (h e) -> p h e", h=H),
                                null_k[:, None, :].to_broadcast((P, H, DH)), ALU.mult).then_inc(s["wqk_ready"], 1)
            eng.wait_ge(s["bias_neg"], 1)
            g.affine_select(out=bias_late, in_=bias_late, compare_op=ALU.is_ge, fill=FAR, base=0,
                            pattern=[[0, H], [-1, P]], channel_multiplier=1).then_inc(s["bias_ready"], 1)

        def pool_general_bias(eng):
            for j in range(QT):
                eng.wait_ge(s["bias_neg"], 2 + j)
                own = bias_all[j][:, :, j * P:(j + 1) * P]
                nc.gpsimd.affine_select(out=own, in_=own, compare_op=ALU.is_ge, fill=FAR, base=0,
                                        pattern=[[0, H], [-1, P]], channel_multiplier=1).then_inc(s["bias_ready"], 1)

        def pool_rstd(eng, L, r, p):
            ts = slice(PART * p, PART * (p + 1))
            eng.wait_ge(s["var_done"], at(r, L.preps, p + 1))
            nc.gpsimd.tensor_tensor(rstd[:, ts], mv[:, ts, 1], half[:, ts], ALU.pow).then_inc(s["rstd_done"], 1)

        def pool_mask(eng, u):
            t, h0, per = LATE.units[u]
            if u >= 8:
                eng.wait_ge(s["scores_done"], u - 7)
            nc.gpsimd.tensor_tensor(bias_masked[:, t % 2, h0:h0 + per, :], bias_late[:, h0:h0 + per, :],
                                    mask_late[:, t:t + 1, :].to_broadcast((P, per, P)), ALU.add).then_inc(s["bias_masked_ready"], 1)

        def pool_late_start(eng):
            pool_rstd(eng, LATE, 0, 0)
            pool_rstd(eng, LATE, 0, 1)
            pool_null_key(eng)
            eng.wait_ge(s["bias_ready"], 1)
            eng.wait_ge(s["mask_ready"], 1)
            for u in range(4):
                pool_mask(eng, u)

        def pool_round(eng, L, r):
            g = nc.gpsimd
            if L.late:
                eng.wait_ge(s["small_in"], SMALL)
            for n in range(L.steps):
                for name, t, hf in L.at(n):
                    i = 2 * t + hf
                    if name == "den":
                        if i >= 2:
                            eng.wait_ge(s["attn_done"], at(r, 2 * L.tiles, i - 1))
                        eng.wait_ge(s["p0n_done"], at(r, 2 * L.tiles, i + 1))
                        g.tensor_tensor(null_part[:, hf, :].rearrange("p (h e) -> p h e", h=8),
                                        small[:, 3, hf, :].unsqueeze(2).to_broadcast((P, 8, DH)),
                                        null_v[:, None, :].to_broadcast((P, 8, DH)), ALU.mult).then_inc(s["null_part_done"], 1)
                    if name == "ctx":
                        eng.wait_ge(s["null_part_done"], at(r, 2 * L.tiles, i + 1))
                        eng.wait_ge(s["attn_mul_done"], at(r, 2 * L.tiles, i + 1))
                        g.tensor_tensor(attn[:, hf, :], attn[:, hf, :], null_part[:, hf, :], ALU.add).then_inc(s["attn_done"], 1)
                    if name == "stat":
                        k = t + L.first_side
                        eng.wait_ge(s["ovar_done"], at(r, L.sides, k + 1))
                        g.tensor_tensor(orstd[:, :], omv[:, 1:2], half[:, 0:1], ALU.pow).then_inc(s["orstd_done"], 1)
                if L.late and n + 4 < L.nu:
                    pool_mask(eng, n + 4)

        def dve_flag(eng):
            v = nc.vector
            words = mask_row.rearrange("a b n -> a (b n)").bitcast(I32).rearrange("a (b n) -> a b n", b=B)
            eng.wait_ge(s["mask_in"], 16)
            v.tensor_reduce(flag_f[0:1, :], words[:, :, 0:(QT - 1) * P // 4], axis=AX.XY, op=ALU.max).then_inc(s["flag_max"], 1)
            eng.wait_ge(s["flag_max"], 1)
            v.tensor_scalar(flag[0:1, :], flag_f[0:1, :], 1.0, None, ALU.min).then_inc(s["flag_ready"], 1)

        def dve_wkv(eng):
            v = nc.vector
            eng.wait_ge(s["g_in_in"], 16)
            eng.wait_ge(s["wkv_in"], 16)
            for c in range(DC):
                v.tensor_scalar(wkk[:, c, 0:DH], wkv_raw[:, c, 0:DH], g_in[:, c:c + 1], None, ALU.mult)
                v.tensor_scalar(wkk[:, c, DH:P], wkv_raw[:, c, 0:DH], g_in[:, c:c + 1], None, ALU.mult)
                last = v.tensor_scalar(wvn[:, c, 0:DH], wkv_raw[:, c, DH:P], g_in[:, c:c + 1], None, ALU.mult)
            last.then_inc(s["wkk_ready"], 1)

        def dve_wq(eng):
            eng.wait_ge(s["wq_in"], 16)
            for c in range(DC):
                nc.vector.tensor_scalar(wq[:, c, :], wq[:, c, :], g_in[:, c:c + 1], -SCALE, ALU.mult, ALU.mult).then_inc(s["wq_scaled"], 1)

        def dve_bias(eng):
            eng.wait_ge(s["bias_in"], 16)
            nc.vector.tensor_scalar(bias_late, bias_late, -1.0, None, ALU.mult).then_inc(s["bias_neg"], 1)

        def dve_mask_late(eng):
            eng.wait_ge(s["mask_late_in"], 16)
            nc.vector.tensor_scalar(mask_late, mask_late_raw, -FAR, FAR, ALU.mult, ALU.add).then_inc(s["mask_ready"], 1)

        def dve_null_q(eng):
            for c in range(DC):
                eng.wait_ge(s["wqk_ready"], c + 1)
                nc.vector.tensor_reduce(wvn[:, c, DH:DH + H], wqk[:, c, :, :], axis=AX.X, op=ALU.add).then_inc(s["null_q_ready"], 1)
            eng.wait_ge(s["small_in"], SMALL)

        def dve_wcat(eng):
            v = nc.vector
            v.tensor_copy(null_ctx[:, :], null_vt[:, 0:1].to_broadcast((P, P))).then_inc(s["null_ctx_ready"], 1)
            for c, bk in enumerate((o_bank, f_bank)):
                eng.wait_ge(s[f"ffn_ps{c}"], 1)
                v.tensor_scalar(wcat[:, c, :], bk[:, 0:FW], g_out[:, c:c + 1], None, ALU.mult).then_inc(s["wcat_ready"], 1)

        def dve_vcat(eng):
            eng.wait_ge(s["vcat_ps"], 1)
            nc.vector.tensor_scalar(vcat[:, :], o_bank[:, 0:D], 1.0 / R, None, ALU.mult).then_inc(s["vcat_ready"], 1)

        def dve_wo_sum(eng):
            eng.wait_ge(s["wo_in"], 16)
            nc.vector.tensor_reduce(wo_sum, wo[:, :, :].rearrange("p m n -> p n m"), axis=AX.X, op=ALU.add).then_inc(s["wo_sum_ready"], 1)

        def dve_general_setup(eng):
            v = nc.vector
            dve_wkv(eng)
            dve_wq(eng)
            dve_bias(eng)
            dve_null_q(eng)
            v.memset(mask_room[:, :], 0.0).then_inc(s["mask_zero"], 1)
            eng.wait_ge(s["mask_zero"], 1)
            v.tensor_scalar(mask_far[0:1, :, :], mask_row[:, :, :], -FAR, FAR, ALU.mult, ALU.add).then_inc(s["mask_ready"], 1)
            for k in range(2):
                eng.wait_ge(s[f"x_late_in{k}"], 16)
            eng.wait_ge(s["x_rest_in"], 16 * B)

        def dve_general_bias(eng):
            for j in range(QT):
                eng.wait_ge(s[f"bias_in{j}"], 16)
                nc.vector.tensor_scalar(bias_all[j], bias_all[j], -1.0, None, ALU.mult).then_inc(s["bias_neg"], 1)

        def dve_stats(eng, L, r, p):
            v = nc.vector
            ts = range(PART * p, PART * (p + 1))
            if L.late:
                eng.wait_ge(s[f"x_late_in{p}"], 16)
            for t in ts:
                xin = x_all[:, t, QT - 1, :] if L.late else x_all[:, r, t, :]
                v.bn_stats(stat[:, t, :], xin).then_inc(s["stats_done"], 1)
            for t in ts:
                eng.wait_ge(s["stats_done"], at(r, L.tiles, t + 1))
                held(eng, r)
                v.bn_aggr(mv[:, t, :], stat[:, t, :]).then_inc(s["mv_done"], 1)
            eng.wait_ge(s["mv_done"], at(r, L.tiles, ts[-1] + 1))
            v.tensor_scalar(mv[:, ts[0]:ts[-1] + 1, 1], mv[:, ts[0]:ts[-1] + 1, 1], EPS, None, ALU.add).then_inc(s["var_done"], 1)

        def dve_norm(eng, L, r, p):
            v = nc.vector
            eng.wait_ge(s["rstd_done"], at(r, L.preps, p + 1))
            for t in range(PART * p, PART * (p + 1)):
                xin = x_all[:, t, QT - 1, :] if L.late else x_all[:, r, t, :]
                v.tensor_scalar(xn_of(L, t), xin, mv[:, t, 0:1], rstd[:, t:t + 1], ALU.subtract, ALU.mult).then_inc(s["xn_done"], 1)

        def dve_rows(eng, L, r, p):
            eng.wait_ge(s["xnt_ps"], at(r, 2 * L.preps, 2 * p + 1))
            nc.vector.tensor_copy(xn_t_of(p)[:, 0, :], xn_banks[0][:, :]).then_inc(s["xnt_dve"], 1)

        def dve_project(eng, L, r, p, between=()):
            v = nc.vector
            for m in range(1, MC, 2):
                eng.wait_ge(s["q_ps"], at(r, MC * L.preps, MC * p + m + 1))
                v.tensor_copy(q_of(p)[:, m, :], q_banks[m % 4][:, :]).then_inc(s["q_dve"], 1)
                if m // 2 < len(between):
                    between[m // 2](eng)
            eng.wait_ge(s["v_ps"], at(r, L.preps, p + 1))
            both = c_bank[1][:, 0:PART * (DH + H)].rearrange("p (j n) -> p j n", j=PART)
            v.tensor_copy(v_all[:, p, :, :], both[:, :, 0:DH])
            v.tensor_tensor(ns_all[:, p, :, :], both[:, :, DH:], null_bias[:, None, :].to_broadcast((P, PART, H)),
                            ALU.subtract).then_inc(s["v_done"], 1)

        def dve_late_start(eng):
            dve_stats(eng, LATE, 0, 0)
            dve_wkv(eng)
            dve_norm(eng, LATE, 0, 0)
            dve_rows(eng, LATE, 0, 0)
            dve_wq(eng)
            dve_stats(eng, LATE, 0, 1)
            dve_norm(eng, LATE, 0, 1)
            dve_project(eng, LATE, 0, 0, (dve_null_q, lambda e: (dve_rows(e, LATE, 0, 1), dve_mask_late(e)), dve_bias, nothing_for))
            dve_wcat(eng)
            dve_project(eng, LATE, 0, 1, (nothing_for, dve_vcat, dve_wo_sum, nothing_for))

        def dve_rest(eng, b):
            if b == 0:
                eng.wait_ge(s["f_read"], f_use(LATE, ("lora", -1, 0)) + 1)
                eng.wait_ge(s["x_rest_in"], 16 * B)
            part = x_all[:, b, 0:QT - 1, :]
            nc.vector.tensor_tensor(part, part, y_null[:, None, :].to_broadcast((P, QT - 1, D)),
                                    ALU.add).then_inc(s["rest_done"], 1)

        def dve_round(eng, L, r):
            v = nc.vector
            for n in range(L.steps):
                for name, t, hf in L.at(n):
                    k = t + L.first_side
                    if name == "norm":
                        eng.wait_ge(s["orstd_done"], at(r, L.sides, k + 1))
                        v.tensor_scalar(xt[:, :], o_bank[:, 0:D], omv[:, 0:1], orstd[:, 0:1],
                                        ALU.subtract, ALU.mult).then_inc(s["xt_done"], 1)
                    if name == "base":
                        use = f_use(L, ("ffn", t, 0))
                        eng.wait_ge(s["f_ps"], at(r, len(L.f_uses), use + 1))
                        v.tensor_copy(lora_in_of(L, t, 1)[:, 0, :], f_bank[:, D:FW]).then_inc(s["lora_in_done"], 1)
                        if t < 0:
                            v.tensor_copy(y_null[:, :], f_bank[:, 0:D]).then_inc(s["f_read"], 1)
                        else:
                            row = x_all[:, t, QT - 1, :] if L.late else x_all[:, r, t, :]
                            v.tensor_tensor(row, f_bank[:, 0:D], row, ALU.add).then_inc(s["f_read"], 1)
                    if name == "fin":
                        kb, pair = L.pairs[hf]
                        use = f_use(L, ("lora", t, hf))
                        eng.wait_ge(s["f_read"], at(r, len(L.f_uses), f_use(L, ("ffn", pair[-1], 0)) + 1))
                        eng.wait_ge(s["f_ps"], at(r, len(L.f_uses), use + 1))
                        t0, nt = pair[0], len(pair)
                        if t0 < 0:
                            row = y_null[:, None, :]
                        else:
                            row = x_all[:, t0:t0 + nt, QT - 1, :] if L.late else x_all[:, r, t0:t0 + nt, :]
                        v.tensor_tensor(row, f_bank[:, 0:nt * D].rearrange("p (b d) -> p b d", b=nt), row, ALU.add).then_inc(s["f_read"], 1)
                if n < L.nu:
                    t, h0, per = L.units[n]
                    nk = L.nk[t]
                    if n >= 3:
                        eng.wait_ge(s["t_ps"], at(r, L.nu, n - 2))
                    if n == 0:
                        eng.wait_ge(s["v_done"], at(r, L.preps, L.preps))
                        if not L.late:
                            eng.wait_ge(s["bias_ready"], 1 + QT)
                    if L.late:
                        eng.wait_ge(s["bias_masked_ready"], n + 1)
                    eng.wait_ge(s["s_ps"], at(r, L.nu, n + 1))
                    held(eng, r)
                    for i in range(per):
                        h = h0 + i
                        bias = bias_masked[:, t % 2, h, :] if L.late else bias_all[t][:, h, :]
                        last = v.tensor_tensor_reduce(
                            out=probs[:, n % 3, i * nk:(i + 1) * nk], in0=s_bank[n % 2][:, i * nk:(i + 1) * nk],
                            in1=bias, scale=1.0, scalar=ns_all[:, t // PART, t % PART, h:h + 1], op0=ALU.add,
                            op1=ALU.min, accum_out=neg_max[:, t % 2, h:h + 1])
                    last.then_inc(s["scores_done"], 1)
                for name, t, hf in L.at(n):
                    i, k, piece = 2 * t + hf, t + L.first_side, (name, t, hf)
                    hs = slice(8 * hf, 8 * hf + 8)
                    if name == "delta":
                        eng.wait_ge(s["scores_done"], at(r, L.nu, L.last_unit[t, hf] + 1))
                        v.tensor_tensor(small[:, 0, hf, :], neg_max[:, t % 2, hs], ns_all[:, t // PART, t % PART, hs],
                                        ALU.subtract).then_inc(s["delta_done"], 1)
                    if name == "den":
                        eng.wait_ge(s["p0_done"], at(r, 2 * L.tiles, i + 1))
                        eng.wait_ge(s["exp_done"], at(r, L.nu, L.last_unit[t, hf] + 1))
                        v.tensor_tensor(small[:, 2, hf, :], small[:, 1, hf, :], sums[:, t % 2, hs], ALU.add).then_inc(s["den_done"], 1)
                        eng.wait_ge(s["den_done"], at(r, 2 * L.tiles, i + 1))
                        v.reciprocal(small[:, 4, hf, :], small[:, 2, hf, :]).then_inc(s["rden_done"], 1)
                        eng.wait_ge(s["rden_done"], at(r, 2 * L.tiles, i + 1))
                        v.tensor_tensor(small[:, 3, hf, :], small[:, 1, hf, :], small[:, 4, hf, :], ALU.mult).then_inc(s["p0n_done"], 1)
                    if name == "ctx":
                        eng.wait_ge(s["pv_done"], at(r, L.nu, L.last_unit[t, hf] + 1))
                        if t:
                            eng.wait_ge(s["x_ps"], at(r, len(L.x_uses), x_use(L, ("turn", t - 1, hf)) + 1))
                        v.tensor_tensor(attn[:, hf, :].rearrange("p (h e) -> p h e", h=8),
                                        c_bank[hf][:, :].rearrange("p (h e) -> p h e", h=8),
                                        small[:, 4, hf, :].unsqueeze(2).to_broadcast((P, 8, DH)), ALU.mult).then_inc(s["attn_mul_done"], 1)
                    if name == "stat":
                        eng.wait_ge(s["o_ps"], at(r, L.sides, k + 1))
                        v.bn_stats(ostat[:, :], o_bank[:, 0:D]).then_inc(s["ostat_done"], 1)
                        eng.wait_ge(s["ostat_done"], at(r, L.sides, k + 1))
                        held(eng, r)
                        v.bn_aggr(omv[:, :], ostat[:, :]).then_inc(s["omv_done"], 1)
                        eng.wait_ge(s["omv_done"], at(r, L.sides, k + 1))
                        v.tensor_scalar(omv[:, 1:2], omv[:, 1:2], EPS, None, ALU.add).then_inc(s["ovar_done"], 1)
                    if name in ("gmax", "gate"):
                        batch = L.batches[hf]
                        nt = len(batch)
                        lin = lora_in_of(L, batch[0], nt)
                        wide = gate_1[:, :, 0:nt].unsqueeze(3)
                    if name == "gmax":
                        eng.wait_ge(s["lora_in_done"], at(r, L.sides, L.first_side + batch[-1] + 1))
                        v.tensor_reduce(gate_1[:, 0, 0:nt], lin[:, :, E * R:], axis=AX.X, op=ALU.max).then_inc(s["gmax_done"], 1)
                        eng.wait_ge(s["gmax_done"], at(r, len(L.batches), hf + 1))
                        v.tensor_tensor(gate_s[:, 0, 0:nt, :], lin[:, :, E * R:], wide[:, 0].to_broadcast((P, nt, E)),
                                        ALU.subtract).then_inc(s["gsub_done"], 1)
                    if name == "gate":
                        eng.wait_ge(s["gexp_done"], at(r, len(L.batches), hf + 1))
                        v.tensor_reduce(gate_1[:, 1, 0:nt], gate_s[:, 1, 0:nt, :], axis=AX.X, op=ALU.add).then_inc(s["gsum_done"], 1)
                        eng.wait_ge(s["gsum_done"], at(r, len(L.batches), hf + 1))
                        v.reciprocal(gate_1[:, 2, 0:nt], gate_1[:, 1, 0:nt]).then_inc(s["grec_done"], 1)
                        eng.wait_ge(s["grec_done"], at(r, len(L.batches), hf + 1))
                        v.tensor_tensor(gate_s[:, 0, 0:nt, :], gate_s[:, 1, 0:nt, :], wide[:, 2].to_broadcast((P, nt, E)),
                                        ALU.mult).then_inc(s["gate_done"], 1)
                        eng.wait_ge(s["gate_done"], at(r, len(L.batches), hf + 1))
                        for b in range(nt):
                            last = v.tensor_tensor(tg[:, b, :].rearrange("p (e q) -> p e q", e=E),
                                                   lin[:, b, 0:E * R].rearrange("p (e q) -> p e q", e=E),
                                                   gate_s[:, 0, b, :].unsqueeze(2).to_broadcast((P, E, R)), ALU.mult)
                        last.then_inc(s["tg_done"], 1)

                if L.late and 12 <= n < 12 + B:
                    dve_rest(eng, n - 12)

        def act_round(eng, L, r):
            a = nc.scalar
            def rows(p):
                eng.wait_ge(s["xnt_ps"], at(r, 2 * L.preps, 2 * p + 2))
                a.activation(xn_t_of(p)[:, 1, :], xn_banks[1][:, :], ACT.Copy).then_inc(s["xnt_act"], 1)

            rows(0)
            for p in range(L.preps):
                eng.wait_ge(s["k_ps"], at(r, L.preps, p + 1))
                a.activation(kt_of(p)[0:DH, 0, :], c_bank[0][0:DH, :], ACT.Copy)
                a.activation(kt_of(p)[DH:P, 1, :], c_bank[0][DH:P, :], ACT.Copy).then_inc(s["kt_done"], 1)
                for m in range(0, MC, 2):
                    eng.wait_ge(s["q_ps"], at(r, MC * L.preps, MC * p + m + 1))
                    a.activation(q_of(p)[:, m, :], q_banks[m % 4][:, :], ACT.Copy).then_inc(s["q_act"], 1)
                    if m == 2 and p + 1 < L.preps:
                        rows(p + 1)

            for n in range(L.steps):
                for piece in L.at(n - 1):
                    name, t, hf = piece
                    if name in ("turn", "xtt", "tgt"):
                        eng.wait_ge(s["x_ps"], at(r, len(L.x_uses), x_use(L, piece) + 1))
                        if name == "turn":
                            to, w = attn_t[:, 4 * hf:4 * hf + 4, :], 4
                        elif name == "xtt":
                            to, w = xt_t[:, :, :], DC
                        else:
                            w = len(L.batches[hf])
                            to = tg_t[:, 0:w, :]
                        a.activation(to, x_bank[:, 0:w * P].rearrange("p (m q) -> p m q", m=w), ACT.Copy).then_inc(s["x_read"], 1)
                if 2 <= n < L.nu + 2:
                    u = n - 2
                    w = L.units[u][2] * L.nk[L.units[u][0]]
                    if u >= 2:
                        eng.wait_ge(s["pv_done"], at(r, L.nu, u - 1))
                    eng.wait_ge(s["t_ps"], at(r, L.nu, u + 1))
                    a.activation(probs_t[:, u % 2, 0:w], t_bank[:, 0:w], ACT.Copy).then_inc(s["probs_t_done"], 1)
                if n < L.nu:
                    t, h0, per = L.units[n]
                    nk = L.nk[t]
                    eng.wait_ge(s["scores_done"], at(r, L.nu, n + 1))
                    for i in range(per):
                        h = h0 + i
                        slot = probs[:, n % 3, i * nk:(i + 1) * nk]
                        last = a.activation(slot, slot, ACT.Exp, bias=neg_max[:, t % 2, h:h + 1], scale=-1.0,
                                            accum_out=sums[:, t % 2, h:h + 1])
                    last.then_inc(s["exp_done"], 1)
                for name, t, hf in L.at(n):
                    i, k, piece = 2 * t + hf, t + L.first_side, (name, t, hf)
                    if name == "p0":
                        eng.wait_ge(s["delta_done"], at(r, 2 * L.tiles, i + 1))
                        a.activation(small[:, 1, hf, :], small[:, 0, hf, :], ACT.Exp).then_inc(s["p0_done"], 1)
                    if name == "gexp":
                        nt = len(L.batches[hf])
                        eng.wait_ge(s["gsub_done"], at(r, len(L.batches), hf + 1))
                        a.activation(gate_s[:, 1, 0:nt, :], gate_s[:, 0, 0:nt, :], ACT.Exp).then_inc(s["gexp_done"], 1)

        def pe_warm(eng):
            eng.wait_ge(s["ident_ready"], 1)
            for _ in range(WARM):
                nc.tensor.matmul(t_bank[:, 0:P], ident[:, :], ident[:, :], start=True, stop=True)

        def pe_wcat(eng, L):
            pe = nc.tensor
            eng.wait_ge(s["ffn_in"], 16 * 5)
            eng.wait_ge(s["xnt_dve"], L.preps)
            eng.wait_ge(s["xnt_act"], L.preps)
            for c, bk in enumerate((o_bank, f_bank)):
                cols = slice(c * P, (c + 1) * P)
                for o2 in range(2):
                    pe.transpose(bk[:, o2 * P:(o2 + 1) * P], w_raw[:, o2, cols], ident[:, :])
                pe.transpose(bk[:, D:D + P], u_raw[:, cols], ident[:, :])
                pe.transpose(bk[:, D + P:FW], gate_raw[0:E, cols], ident[0:E, 0:E]).then_inc(s[f"ffn_ps{c}"], 1)

        def pe_vcat(eng):
            pe = nc.tensor
            eng.wait_ge(s["wcat_ready"], 1)
            pe.transpose(o_bank[:, 0:P], v_raw[:, 0, :], ident[:, :])
            pe.transpose(o_bank[:, P:D], v_raw[:, 1, :], ident[:, :]).then_inc(s["vcat_ps"], 1)

        def pe_turn_rows(eng, L, r, p):
            pe = nc.tensor
            if p:
                eng.wait_ge(s["xnt_dve"], at(r, L.preps, p))
                eng.wait_ge(s["xnt_act"], at(r, L.preps, p))
            for c in range(DC):
                for j in range(PART):
                    if c == 0:
                        eng.wait_ge(s["xn_done"], at(r, L.tiles, PART * p + j + 1))
                    last = pe.transpose(xn_banks[c][:, j * P:(j + 1) * P], xn_of(L, PART * p + j)[:, c * P:(c + 1) * P], ident[:, :])
                last.then_inc(s["xnt_ps"], 1)

        def pe_keys(eng, L, r, p, first):
            eng.wait_ge(s["xnt_dve"], at(r, L.preps, p + 1))
            eng.wait_ge(s["xnt_act"], at(r, L.preps, p + 1))
            if first and p == 0:
                eng.wait_ge(s["wkk_ready"], 1)
            if p:
                eng.wait_ge(s["kt_done"], at(r, L.preps, p))
            for c in range(DC):
                last = nc.tensor.matmul(c_bank[0][:, :], wkk[:, c, :], xn_t_of(p)[:, c, :], start=(c == 0), stop=(c == DC - 1))
            last.then_inc(s["k_ps"], 1)

        def pe_queries(eng, L, r, p, ms, first):
            for m in ms:
                if m >= 4 or p:
                    eng.wait_ge(s["q_dve" if m % 2 else "q_act"], at(r, 4 * L.preps, 4 * p + m // 2 - 1))
                for c in range(DC):
                    if first and p == 0 and m == 0:
                        eng.wait_ge(s["wq_scaled"], c + 1)
                    last = nc.tensor.matmul(q_banks[m % 4][:, :], wq[:, c, m * P:(m + 1) * P], xn_t_of(p)[:, c, :],
                                            start=(c == 0), stop=(c == DC - 1))
                last.then_inc(s["q_ps"], 1)

        def pe_values(eng, L, r, p, first):
            if first and p == 0:
                eng.wait_ge(s["null_q_ready"], DC)
            if p:
                eng.wait_ge(s["v_done"], at(r, L.preps, p))
            for j in range(PART):
                for c in range(DC):
                    last = nc.tensor.matmul(c_bank[1][:, j * (DH + H):(j + 1) * (DH + H)], xn_t_of(p)[:, c, j * P:(j + 1) * P],
                                            wvn[:, c, :], start=(c == 0), stop=(c == DC - 1))
            last.then_inc(s["v_ps"], 1)

        def pe_project(eng, L, r, first):
            for p in range(L.preps):
                if p == 0:
                    pe_turn_rows(eng, L, r, 0)
                pe_keys(eng, L, r, p, first)
                pe_queries(eng, L, r, p, range(MC // 2), first)
                if p + 1 < L.preps:
                    pe_turn_rows(eng, L, r, p + 1)
                if first and p == L.preps - 1:
                    pe_vcat(eng) if L.late else None
                pe_queries(eng, L, r, p, range(MC // 2, MC), first)
                pe_values(eng, L, r, p, first)
                if first and p == 0:
                    pe_wcat(eng, L)
            if first and not L.late:
                pe_vcat(eng)

        def pe_round(eng, L, r, first):
            pe = nc.tensor
            eng.wait_ge(s["q_act"], at(r, 4 * L.preps, 4 * L.preps))
            eng.wait_ge(s["q_dve"], at(r, 4 * L.preps, 4 * L.preps))
            eng.wait_ge(s["kt_done"], at(r, L.preps, L.preps))
            eng.wait_ge(s["v_done"], at(r, L.preps, L.preps))
            if first:
                if not L.late:
                    eng.wait_ge(s["mask_ready"], 1)
                eng.wait_ge(s["consts_ready"], 2)
                eng.wait_ge(s["null_ctx_ready"], 1)
                eng.wait_ge(s["vcat_ready"], 1)
                eng.wait_ge(s["wcat_ready"], 2)
                eng.wait_ge(s["wo_in"], 16)

            def free_x(piece):
                if x_use(L, piece):
                    eng.wait_ge(s["x_read"], at(r, len(L.x_uses), x_use(L, piece)))

            def free_f(piece):
                if f_use(L, piece):
                    eng.wait_ge(s["f_read"], at(r, len(L.f_uses), f_use(L, piece)))

            for n in range(L.steps):
                if n < L.nu:
                    t, h0, per = L.units[n]
                    nk, k0, p, j = L.nk[t], L.k0[t], t // PART, t % PART
                    bk = s_bank[n % 2]
                    if n >= 2:
                        eng.wait_ge(s["scores_done"], at(r, L.nu, n - 1))
                    if not L.late:
                        pe.matmul(bk[:, 0:per * nk], pick[:, :], mask_far[:, r, 0:nk].unsqueeze(1).to_broadcast((P, per, nk)),
                                  start=True, stop=False)
                    if per == 1:
                        last = pe.matmul(bk[:, 0:nk], q_of(p)[:, h0 // 2, j * P:(j + 1) * P],
                                         kt_of(p)[:, h0 % 2, k0:k0 + nk], start=False, stop=True)
                    else:
                        for i in range(0, per, 2):
                            last = pe.matmul(bk[:, i * nk:(i + 2) * nk].rearrange("p (e k) -> p e k", e=2),
                                             q_of(p)[:, (h0 + i) // 2, j * P:(j + 1) * P],
                                             kt_of(p)[:, :, k0:k0 + nk], start=L.late, stop=(L.late or i == per - 2))
                    last.then_inc(s["s_ps"], 1)
                if 2 <= n < L.nu + 2:
                    u = n - 2
                    t, h0, per = L.units[u]
                    if u >= 1:
                        eng.wait_ge(s["probs_t_done"], at(r, L.nu, u))
                    eng.wait_ge(s["exp_done"], at(r, L.nu, u + 1))
                    for i in range(per * L.nk[t] // P):
                        last = pe.transpose(t_bank[:, i * P:(i + 1) * P], probs[:, u % 3, i * P:(i + 1) * P], ident[:, :])
                    last.then_inc(s["t_ps"], 1)
                if 3 <= n < L.nu + 3:
                    u = n - 3
                    t, h0, per = L.units[u]
                    nb = L.nk[t] // P
                    if h0 % 8 == 0 and t:
                        eng.wait_ge(s["attn_mul_done"], at(r, 2 * L.tiles, 2 * (t - 1) + h0 // 8 + 1))
                    eng.wait_ge(s["probs_t_done"], at(r, L.nu, u + 1))
                    for i in range(per):
                        h = h0 + i
                        for kb in range(nb):
                            last = pe.matmul(c_bank[h // 8][:, (h % 8) * DH:(h % 8 + 1) * DH],
                                             probs_t[:, u % 2, (i * nb + kb) * P:(i * nb + kb + 1) * P],
                                             v_all[:, t // PART, L.k0[t] // P + kb, :], start=(kb == 0), stop=(kb == nb - 1))
                    last.then_inc(s["pv_done"], 1)
                for name, t, hf in L.at(n):
                    i, k, piece = 2 * t + hf, t + L.first_side, (name, t, hf)
                    if name == "turn":
                        free_x(piece)
                        eng.wait_ge(s["attn_done"], at(r, 2 * L.tiles, i + 1))
                        for m in range(4):
                            last = pe.transpose(x_bank[:, m * P:(m + 1) * P], attn[:, hf, m * P:(m + 1) * P], ident[:, :])
                        last.then_inc(s["x_ps"], 1)
                    if name in ("out", "out_end"):
                        if t >= 0:
                            eng.wait_ge(s["x_read"], at(r, len(L.x_uses), x_use(L, ("turn", t, name == "out_end")) + 1))
                        if name == "out" and k:
                            eng.wait_ge(s["xt_done"], at(r, L.sides, k))
                        if t < 0:
                            ms = ()
                            if name == "out_end":
                                eng.wait_ge(s["wo_sum_ready"], 1)
                                last = pe.matmul(o_bank[:, 0:D], null_ctx[:, :], wo_sum, start=True, stop=True)
                        else:
                            ms = range(4) if name == "out" else range(4, MC)
                        for m in ms:
                            last = pe.matmul(o_bank[:, 0:D], attn_t[:, m, :], wo[:, m, :], start=(m == 0), stop=(m == MC - 1))
                        if name == "out_end":
                            last.then_inc(s["o_ps"], 1)
                    if name == "xtt":
                        free_x(piece)
                        eng.wait_ge(s["xt_done"], at(r, L.sides, k + 1))
                        for c in range(DC):
                            last = pe.transpose(x_bank[:, c * P:(c + 1) * P], xt[:, c * P:(c + 1) * P], ident[:, :])
                        last.then_inc(s["x_ps"], 1)
                    if name == "ffn":
                        free_f(piece)
                        eng.wait_ge(s["x_read"], at(r, len(L.x_uses), x_use(L, ("xtt", t, 0)) + 1))
                        for c in range(DC):
                            last = pe.matmul(f_bank[:, 0:FW], xt_t[:, c, :], wcat[:, c, :], start=(c == 0), stop=(c == DC - 1))
                        last.then_inc(s["f_ps"], 1)
                    if name == "tgt":
                        free_x(piece)
                        eng.wait_ge(s["tg_done"], at(r, len(L.batches), hf + 1))
                        for b in range(len(L.batches[hf])):
                            last = pe.transpose(x_bank[:, b * P:(b + 1) * P], tg[:, b, :], ident[:, :])
                        last.then_inc(s["x_ps"], 1)
                    if name == "lora":
                        kb, pair = L.pairs[hf]
                        free_f(piece)
                        eng.wait_ge(s["x_read"], at(r, len(L.x_uses), x_use(L, ("tgt", t, kb)) + 1))
                        for b, tile in enumerate(pair):
                            last = pe.matmul(f_bank[:, b * D:(b + 1) * D], tg_t[:, L.batches[kb].index(tile), :], vcat[:, :],
                                             start=True, stop=True)
                        last.then_inc(s["f_ps"], 1)

        LATE, ALL = Layout(True), Layout(False)

        def sp_general_bias(eng):
            eng.wait_ge(s["bias_ready"], 1)
            eng.wait_ge(s["vcat_ready"], 1)
            eng.wait_ge(s["null_q_ready"], DC)
            eng.wait_ge(s["mask_late_in"], 16)
            eng.wait_ge(s["consts_ready"], 2)
            for j in range(QT):
                eng.dma_start(bias_all[j], bias_d[:, j * P:(j + 1) * P, 0:(j + 1) * P]
                              .rearrange("h p k -> p h k")).then_inc(s[f"bias_in{j}"], 16)

        def sp_round(eng, L, r):
            if L.late:
                for b in range(B):
                    eng.wait_ge(s["rest_done"], b + 1)
                    eng.dma_start(out_d[b, 0:(QT - 1) * P, :].rearrange("(t p) d -> p t d", p=P),
                                  x_all[:, b, 0:QT - 1, :]).then_inc(s["stored"], 16)
            for name, t, hf in L.f_uses:
                if name == "ffn" or t < 0:
                    continue
                eng.wait_ge(s["f_read"], at(r, len(L.f_uses), f_use(L, (name, t, hf)) + 1))
                t0, nt = L.pairs[hf][1][0], len(L.pairs[hf][1])
                if L.late:
                    eng.dma_start(out_d[t0:t0 + nt, (QT - 1) * P:, :].rearrange("t p d -> p t d"),
                                  x_all[:, t0:t0 + nt, QT - 1, :]).then_inc(s["stored"], 16)
                else:
                    rows = out_d[bass.ds(r, 1), t0 * P:(t0 + nt) * P, :]
                    eng.dma_start(rows.rearrange("a (t p) d -> p (a t) d", p=P),
                                  x_all[:, r, t0:t0 + nt, :]).then_inc(s["stored"], 16)

        def paths(eng, late, general, body, finish=lambda L: None):
            eng.wait_ge(s["flag_ready"], 1)
            early = eng.value_load(flag[0:1, 0:1], min_val=0, max_val=1)
            with eng.If(early == 0):
                late()
                body(LATE, 0, True)
                finish(LATE)
            with eng.Else():
                general()
                body(ALL, 0, True)
                with eng.Fori(1, B) as r:
                    body(ALL, r, False)
                finish(ALL)

        def nothing():
            pass

        def nothing_for(eng):
            pass

        @block.sync
        def _(sp):
            sp_setup(sp)
            paths(sp, nothing, lambda: sp_general_bias(sp), lambda L, r, first: sp_round(sp, L, r),
                  lambda L: sp.wait_ge(s["stored"], 16 * (B + B // 2 if L.late else B * QT // 2)))

        @block.gpsimd
        def _(pool):
            pool_setup(pool)
            paths(pool, lambda: pool_late_start(pool), lambda: pool_null_key(pool),
                  lambda L, r, first: (
                      None if L.late else (pool_rstd(pool, L, r, 0), pool_general_bias(pool) if first else None),
                      pool_round(pool, L, r)))

        @block.scalar
        def _(act):
            act_setup_dma(act)
            paths(act, nothing, nothing, lambda L, r, first: act_round(act, L, r))

        @block.vector
        def _(dve):
            dve_flag(dve)
            paths(dve, lambda: dve_late_start(dve), lambda: dve_general_setup(dve), lambda L, r, first: (
                None if L.late else (dve_stats(dve, L, r, 0), dve_norm(dve, L, r, 0),
                                     dve_rows(dve, L, r, 0), dve_project(dve, L, r, 0),
                                     (dve_wcat(dve), dve_vcat(dve), dve_general_bias(dve)) if first else None),
                dve_round(dve, L, r)))

        @block.tensor
        def _(pe):
            pe_warm(pe)
            paths(pe, nothing, nothing, lambda L, r, first: (
                pe_project(pe, L, r, first), pe_round(pe, L, r, first)))


_INS = ["x", "fside_16xSxS_0", "cond_64", "mask_BxS_bk0", "L0_cond_g_in", "L0_cond_null_attn_bias", "L0_cond_Wq",
        "L0_cond_Wkv", "L0_cond_Wo", "L0_cond_g_out", "L0_ffn_weight", "L0_ffn_gate_w", "L0_ffn_lora_U",
        "L0_ffn_lora_V"]


def kernel(**inputs):
    import numpy as np
    import concourse.bacc as bacc
    from concourse import mybir as mb
    from concourse.bass_utils import run_bass_kernel_spmd

    nc = bacc.Bacc("TRN2", target_bir_lowering=False, num_devices=1)
    arrays, args = {}, []
    for name in _INS:
        a = np.ascontiguousarray(inputs[name])
        arrays[f"in_{name}"] = a
        args.append(nc.dram_tensor(f"in_{name}", a.shape, mb.dt.from_np(a.dtype), kind="ExternalInput").ap())
    args.append(nc.dram_tensor("out", (B, N, D), mb.dt.float32, kind="ExternalOutput").ap())
    attention_ffn(nc, *args)
    r = run_bass_kernel_spmd(nc, [arrays], core_ids=[0])
    return r.results[0]["out"]
```

```python
from contextlib import ExitStack

import concourse.bass as bass
from concourse import mybir

ALU = mybir.AluOpType
ACT = mybir.ActivationFunctionType
AX = mybir.AxisListType
F32 = mybir.dt.float32
BF16 = mybir.dt.bfloat16
U8 = mybir.dt.uint8
I32 = mybir.dt.int32

P = 128
B, N, D = 8, 512, 256
H, DH = 16, 64
INNER = H * DH
DC = D // P
MC = INNER // P
QT = N // P
E, R = 8, 16
EPS = 1e-5
SCALE = DH ** -0.5
FAR = 1e30
FW = D + E * R + E
PART = 4
WARM = 14


class Layout:

    def __init__(self, late):
        self.late = late
        self.preps = 2 if late else 1
        self.tiles = PART * self.preps
        self.nk = [P if late else P * (t + 1) for t in range(self.tiles)]
        self.k0 = [P * (t % PART) if late else 0 for t in range(self.tiles)]
        self.groups = [(0, 1), (2, 3), (4, 5, 6, 7)] if late else [(0, 1, 2, 3)]
        self.units = []
        for t in range(self.tiles):
            per = {P: 4, 2 * P: 2}.get(self.nk[t], 1)
            self.units += [(t, h, per) for h in range(0, H, per)]
        self.nu = len(self.units)
        self.first_side = 1 if late else 0
        self.sides = self.tiles + self.first_side
        self.batches = [[-1], [0, 1, 2, 3], [4, 5], [6], [7]] if late else [[0, 1, 2, 3]]
        self.last_unit = {(t, h // 8): u for u, (t, h, _) in enumerate(self.units)}
        self.side = {}
        u1 = {-1: -7, **{t: self.last_unit[t, 1] for t in range(self.tiles)}}
        for t in range(self.tiles):
            for hf in range(2):
                self.put(self.last_unit[t, hf], HALF_STAGES, t, hf)
        for t in range(-self.first_side, self.tiles):
            self.put(u1[t] - (t == self.tiles - 1), TILE_STAGES, t, 0)
        self.pairs = []
        for k, batch in enumerate(self.batches):
            start, back = u1[batch[-1]], late and batch[-1] == self.tiles - 3
            if late and batch[-1] == self.tiles - 1:
                start -= 2
            self.put(start, BATCH_STAGES, batch[-1], k)
            for m in range(0, len(batch), 2):
                self.put(start + back + 2 * m, PAIR_STAGES, batch[-1], len(self.pairs))
                self.pairs.append((k, batch[m:m + 2]))
        self.early_queries = (MC - 1,) if late else ()
        for i, m in enumerate(self.early_queries):
            self.put(i, ((0, "query"),), 0, m)
        self.steps = max(self.side) + 1
        self.order = [(n, x) for n in range(self.steps) for x in self.side.get(n, ())]
        self.x_uses = [x for _, x in self.order if x[0] in ("turn", "tgt")]
        last = self.tiles - 1
        self.l_uses = [("xtt", last, 0), ("ffn", last, 0)]
        self.f_uses = [x for _, x in self.order if x[0] in ("xtt", "ffn", "lora") and x not in self.l_uses]

    def put(self, start, stages, t, k):
        for lag, name in stages:
            pieces = self.side.setdefault(start + lag, [])
            pieces.append((name, t, k))
            pieces.sort(key=lambda x: (x[1], STAGE_ORDER.index(x[0]), x[2]))

    def at(self, n):
        return self.side.get(n, ())


HALF_STAGES = ((0, "delta"), (1, "p0"), (2, "den"), (4, "ctx"), (6, "turn"))
TILE_STAGES = ((7, "out"), (8, "out_end"), (9, "stat"), (10, "norm"), (11, "xtt"), (12, "ffn"), (13, "base"))
BATCH_STAGES = ((14, "gmax"), (15, "gexp"), (16, "gate"), (17, "tgt"))
PAIR_STAGES = ((18, "lora"), (19, "fin"))
STAGE_ORDER = ["query"] + [name for stages in (HALF_STAGES, TILE_STAGES, BATCH_STAGES, PAIR_STAGES) for _, name in stages]


def attention_ffn(nc, x_d, bias_d, cond_d, mask_d, g_in_d, nb_d, wq_d, wkv_d, wo_d, g_out_d,
                  w_d, gate_d, u_d, v_d, out_d):
    ctx = ExitStack()
    with ctx:
        def sb(name, shape, dt=F32):
            return ctx.enter_context(nc.sbuf_tensor(name, shape, dt))

        def bank(name):
            return ctx.enter_context(nc.psum_tensor(name, [P, 512], F32))

        def sem(name):
            return ctx.enter_context(nc.semaphore(name))

        x_all = sb("x_all", [P, B, QT, D])
        ident = sb("ident", [P, P])
        wq = sb("wq", [P, DC, INNER])
        wkk = sb("wkk", [P, DC, P])
        wvn = sb("wvn", [P, DC, DH + H])
        wo = sb("wo", [P, MC, D])
        wcat = sb("wcat", [P, DC, FW])
        vcat = sb("vcat", [P, D])
        g_in = sb("g_in", [P, DC])
        g_out = sb("g_out", [P, DC])
        null_k = sb("null_k", [P, DH])
        null_v = sb("null_v", [P, DH])
        null_vt = sb("null_vt", [P, 1])
        null_ctx = sb("null_ctx", [P, P])
        null_bias = sb("null_bias", [P, H])
        y_null = sb("y_null", [P, D])
        pick = sb("pick", [P, P], BF16)
        mask_room = sb("mask_room", [P, B * N // 2])
        mask_far = mask_room[:, :].bitcast(BF16).rearrange("p (b n) -> p b n", b=B)
        mask_late = mask_room[:, 0:B * P].rearrange("p (b n) -> p b n", b=B)
        mask_row = sb("mask_row", [1, B, N], U8)
        xn_t = sb("xn_t", [P, DC, N])
        q_all = sb("q_all", [P, MC, N])
        kt_all = sb("kt_all", [P, 2, N])
        v_all = sb("v_all", [P, 2, PART, DH])
        ns_all = sb("ns_all", [P, 2, PART, H])
        probs = sb("probs", [P, 3, 512])
        xn = probs[:, 0:2, :].rearrange("p a (j d) -> p (a j) d", d=D)
        probs_t = sb("probs_t", [P, 2, 512])
        attn = sb("attn", [P, 2, 512])
        null_part = sb("null_part", [P, 2, 512])
        attn_t = sb("attn_t", [P, MC, P])
        xt = sb("xt", [P, D])
        xt_t = sb("xt_t", [P, DC, P])
        tg = sb("tg", [P, PART, E * R])
        tg_t = sb("tg_t", [P, PART, P])
        lora_in = sb("lora_in", [P, PART, FW - D])
        stat = sb("stat", [P, 2 * PART, 6])
        mv = sb("mv", [P, 2 * PART, 2])
        rstd = sb("rstd", [P, 2 * PART])
        half = sb("half", [P, 2 * PART])
        neg_max = sb("neg_max", [P, 2, H])
        sums = sb("sums", [P, 2, H])
        small = sb("small", [P, 5, 2, 8])
        ostat = sb("ostat", [P, 6])
        omv = sb("omv", [P, 2])
        orstd = sb("orstd", [P, 1])
        flag_f = sb("flag_f", [P, 1])
        flag = sb("flag", [P, 1], I32)
        gate_e = sb("gate_e", [P, PART, E])
        gate_1 = sb("gate_1", [P, 3, PART])
        big = sb("big", [P, H * P * (1 + 2 + 3 + 4)])
        starts = [0, H * P, 3 * H * P, 6 * H * P]
        bias_all = [big[:, s:s + H * P * (j + 1)].rearrange("p (h k) -> p h k", h=H)
                    for j, s in enumerate(starts)]
        o = [0]

        def carve(n):
            o[0] += n
            return big[:, o[0] - n:o[0]]

        bias_late = carve(H * P).rearrange("p (h k) -> p h k", h=H)
        q_late = carve(MC * N).rearrange("p (m n) -> p m n", m=MC)
        kt_late = carve(2 * N).rearrange("p (e n) -> p e n", e=2)
        xn_t_late = carve(DC * N).rearrange("p (c n) -> p c n", c=DC)
        wo_sum = carve(D)
        xn_late = carve(PART * D).rearrange("p (j d) -> p j d", j=PART)
        lora_in_late = carve(PART * (FW - D)).rearrange("p (j n) -> p j n", j=PART)
        w_raw = carve(2 * D).rearrange("p (o d) -> p o d", o=2)
        u_raw = carve(D)
        gate_raw = carve(D)
        v_raw = carve(2 * E * R).rearrange("p (o n) -> p o n", o=2)
        wkv_raw = carve(DC * P).rearrange("p (c n) -> p c n", c=DC)
        wqk = carve(DC * INNER).rearrange("p (c h e) -> p c h e", c=DC, h=H)
        mask_late_raw = carve(B * P // 4).bitcast(U8).rearrange("p (b n) -> p b n", b=B)
        bias_masked = carve(2 * H * P).rearrange("p (t h k) -> p t h k", t=2, h=H)

        s_bank = [bank("s_bank0"), bank("s_bank1")]
        t_bank = bank("t_bank")
        c_bank = [bank("c_bank0"), bank("c_bank1")]
        x_bank = bank("x_bank")
        o_bank = bank("o_bank")
        f_bank = bank("f_bank")
        q_banks = s_bank + [t_bank, x_bank]
        xn_banks = [o_bank, f_bank]

        NAMES = """x_late_in0 x_late_in1 x_rest_in wq_in wkv_in small_in mask_in mask_late_in bias_masked_ready
            mask_zero g_in_in null_k_in bias_in bias_in0 bias_in1 bias_in2 bias_in3 wo_in ffn_in ident_zero
            ident_ready consts_ready wq_scaled wkk_ready wqk_ready null_q_ready bias_neg bias_ready mask_ready
            ffn_ps0 ffn_ps1 wcat_ready vcat_ps vcat_ready null_ctx_ready wo_sum_ready stats_done mv_done
            var_done rstd_done xn_done xnt_ps xnt_dve xnt_act k_ps kt_done v_ps v_done q_ps q_act q_dve s_ps
            scores_done exp_done t_ps probs_t_done pv_done delta_done p0_done den_done rden_done p0n_done
            null_part_done attn_mul_done attn_done x_ps x_read l_ps l_read o_ps ostat_done omv_done ovar_done
            orstd_done xt_done f_ps f_read lora_in_done gmax_done gexp_done grec_done tg_done rest_done stored
            wait_taken flag_max flag_ready table_in""".split()
        s = {n: sem(n) for n in NAMES}

        def at(r, per, n):
            return r * per + n

        def held(eng, r):
            if not isinstance(r, int):
                eng.sem_inc(s["wait_taken"], 1)

        def q_of(p):
            return q_late if p else q_all

        def xn_of(L, t):
            return xn_late[:, t - PART, :] if t >= PART else xn[:, t, :]

        def lora_in_of(L, t0, n):
            if t0 >= PART:
                return lora_in_late[:, t0 - PART:t0 - PART + n, :]
            return lora_in[:, max(t0, 0):max(t0, 0) + n, :]

        def slots(batch):
            first = max(batch[0], 0) % PART
            return slice(first, first + len(batch))

        def x_use(L, piece):
            return L.x_uses.index(piece)

        def f_use(L, piece):
            return L.f_uses.index(piece)

        def f_of(L, piece):
            if piece in L.l_uses:
                return s_bank[1], s["l_ps"], s["l_read"], len(L.l_uses), L.l_uses.index(piece)
            return f_bank, s["f_ps"], s["f_read"], len(L.f_uses), L.f_uses.index(piece)

        def o_of(L, t):
            return s_bank[0] if t == L.tiles - 1 else o_bank

        def xn_t_of(p):
            return xn_t_late if p else xn_t

        def kt_of(p):
            return kt_late if p else kt_all

        block = ctx.enter_context(nc.Block())

        def x_late_load(eng, k):
            eng.dma_start(x_all[:, PART * k:PART * (k + 1), QT - 1, :],
                          x_d[PART * k:PART * (k + 1), (QT - 1) * P:, :].rearrange("b p d -> p b d")).then_inc(s[f"x_late_in{k}"], 16)

        def sp_setup(eng):
            eng.dma_start(mask_row.rearrange("a b n -> a (b n)"),
                          mask_d.rearrange("(a b) n -> a (b n)", a=1)).then_inc(s["mask_in"], 16)
            eng.dma_start(wkv_raw, wkv_d.rearrange("(c p) n -> p c n", c=DC)).then_inc(s["wkv_in"], 16)
            eng.dma_start(wq[:, :, :], wq_d.rearrange("(c p) n -> p c n", c=DC)).then_inc(s["wq_in"], 16)
            x_late_load(eng, 1)
            eng.dma_start(bias_late, bias_d[:, (QT - 1) * P:, (QT - 1) * P:]
                          .rearrange("h p k -> p h k")).then_inc(s["bias_in"], 16)
            eng.dma_start(w_raw, w_d.rearrange("(o p) d -> p o d", p=P)).then_inc(s["ffn_in"], 16)
            eng.dma_start(u_raw, u_d.rearrange("e r d -> (e r) d")).then_inc(s["ffn_in"], 16)
            eng.dma_start(gate_raw[0:E, :], gate_d).then_inc(s["ffn_in"], 16)
            for c in range(2):
                eng.dma_start(v_raw[:, c, :].rearrange("p (e r) -> p e r", e=E),
                              v_d[:, c * P:(c + 1) * P, :].rearrange("e p r -> p e r")).then_inc(s["ffn_in"], 16)
            with nc.allow_non_contiguous_dma("a gain and the null value, one word a partition"):
                eng.dma_start(null_bias[:, :], nb_d.rearrange("(a h) -> a h", a=1).to_broadcast((P, H))).then_inc(s["small_in"], 16)
                eng.dma_start(null_v[:, :], cond_d[1:2, :].to_broadcast((P, DH))).then_inc(s["small_in"], 16)
                for e in range(2):
                    eng.dma_start(null_vt[e * DH:(e + 1) * DH, :], cond_d[1:2, :].rearrange("a p -> p a")).then_inc(s["small_in"], 16)
                eng.dma_start(g_out[:, :], g_out_d.rearrange("(c p) -> p c", c=DC)).then_inc(s["small_in"], 16)
            eng.dma_start(wo[:, :, :], wo_d.rearrange("(m p) n -> p m n", m=MC)).then_inc(s["wo_in"], 16)
            for b in range(B):
                eng.dma_start(x_all[:, b, 0:QT - 1, :],
                              x_d[b, 0:(QT - 1) * P, :].rearrange("(t p) d -> p t d", p=P)).then_inc(s["x_rest_in"], 16)

        def act_setup_dma(eng):
            x_late_load(eng, 0)
            with nc.allow_non_contiguous_dma("a gain, one word a partition"):
                eng.dma_start(g_in[:, :], g_in_d.rearrange("(c p) -> p c", c=DC)).then_inc(s["g_in_in"], 16)
                eng.dma_start(null_k[:, :], cond_d[0:1, :].to_broadcast((P, DH))).then_inc(s["null_k_in"], 16)
                eng.dma_start(mask_late_raw, mask_d[:, (QT - 1) * P:].unsqueeze(0).to_broadcast((P, B, P))).then_inc(s["mask_late_in"], 16)

        SMALL = 5 * 16

        def pool_setup(eng):
            g = nc.gpsimd
            g.memset(ident[:, :], 0.0).then_inc(s["ident_zero"], 1)
            eng.wait_ge(s["ident_zero"], 1)
            g.affine_select(out=ident[:, :], in_=ident[:, :], compare_op=ALU.not_equal, fill=1.0, base=0,
                            pattern=[[-1, P]], channel_multiplier=1).then_inc(s["ident_ready"], 1)
            g.memset(pick[:, :], 0.0)
            g.memset(half[:, :], -0.5)
            g.memset(kt_all[:, :, :], 0.0)
            g.memset(kt_late, 0.0).then_inc(s["consts_ready"], 1)
            eng.wait_ge(s["consts_ready"], 1)
            g.memset(pick[0:1, :], 1.0).then_inc(s["consts_ready"], 1)

        def pool_null_key(eng):
            g = nc.gpsimd
            eng.wait_ge(s["null_k_in"], 16)
            for c in range(DC):
                eng.wait_ge(s["wq_scaled"], c + 1)
                g.tensor_tensor(wqk[:, c, :, :], wq[:, c, :].rearrange("p (h e) -> p h e", h=H),
                                null_k[:, None, :].to_broadcast((P, H, DH)), ALU.mult).then_inc(s["wqk_ready"], 1)
            eng.wait_ge(s["bias_neg"], 1)
            g.affine_select(out=bias_late, in_=bias_late, compare_op=ALU.is_ge, fill=FAR, base=0,
                            pattern=[[0, H], [-1, P]], channel_multiplier=1).then_inc(s["bias_ready"], 1)

        def pool_general_bias(eng):
            for j in range(QT):
                eng.wait_ge(s["bias_neg"], 2 + j)
                own = bias_all[j][:, :, j * P:(j + 1) * P]
                nc.gpsimd.affine_select(out=own, in_=own, compare_op=ALU.is_ge, fill=FAR, base=0,
                                        pattern=[[0, H], [-1, P]], channel_multiplier=1).then_inc(s["bias_ready"], 1)

        def pool_rstd(eng, L, r, g):
            ts = slice(L.groups[g][0], L.groups[g][-1] + 1)
            eng.wait_ge(s["var_done"], at(r, len(L.groups), g + 1))
            nc.gpsimd.tensor_tensor(rstd[:, ts], mv[:, ts, 1], half[:, ts], ALU.pow).then_inc(s["rstd_done"], 1)

        def pool_mask(eng, u):
            t, h0, per = LATE.units[u]
            if u >= 8:
                eng.wait_ge(s["scores_done"], u - 7)
            nc.gpsimd.tensor_tensor(bias_masked[:, t % 2, h0:h0 + per, :], bias_late[:, h0:h0 + per, :],
                                    mask_late[:, t:t + 1, :].to_broadcast((P, per, P)), ALU.add).then_inc(s["bias_masked_ready"], 1)

        def pool_late_start(eng):
            for g in range(len(LATE.groups)):
                pool_rstd(eng, LATE, 0, g)
            pool_null_key(eng)
            eng.wait_ge(s["bias_ready"], 1)
            eng.wait_ge(s["mask_ready"], 1)
            for u in range(4):
                pool_mask(eng, u)

        def pool_round(eng, L, r):
            g = nc.gpsimd
            if L.late:
                eng.wait_ge(s["small_in"], SMALL)
            for n in range(L.steps):
                for name, t, hf in L.at(n):
                    i = 2 * t + hf
                    if name == "den":
                        if i >= 2:
                            eng.wait_ge(s["attn_done"], at(r, 2 * L.tiles, i - 1))
                        eng.wait_ge(s["p0n_done"], at(r, 2 * L.tiles, i + 1))
                        g.tensor_tensor(null_part[:, hf, :].rearrange("p (h e) -> p h e", h=8),
                                        small[:, 3, hf, :].unsqueeze(2).to_broadcast((P, 8, DH)),
                                        null_v[:, None, :].to_broadcast((P, 8, DH)), ALU.mult).then_inc(s["null_part_done"], 1)
                    if name == "ctx":
                        eng.wait_ge(s["null_part_done"], at(r, 2 * L.tiles, i + 1))
                        eng.wait_ge(s["attn_mul_done"], at(r, 2 * L.tiles, i + 1))
                        g.tensor_tensor(attn[:, hf, :], attn[:, hf, :], null_part[:, hf, :], ALU.add).then_inc(s["attn_done"], 1)
                    if name == "stat":
                        k = t + L.first_side
                        eng.wait_ge(s["ovar_done"], at(r, L.sides, k + 1))
                        g.tensor_tensor(orstd[:, :], omv[:, 1:2], half[:, 0:1], ALU.pow).then_inc(s["orstd_done"], 1)
                if L.late and n + 4 < L.nu:
                    pool_mask(eng, n + 4)

        def dve_flag(eng):
            v = nc.vector
            words = mask_row.rearrange("a b n -> a (b n)").bitcast(I32).rearrange("a (b n) -> a b n", b=B)
            eng.wait_ge(s["mask_in"], 16)
            v.tensor_reduce(flag_f[0:1, :], words[:, :, 0:(QT - 1) * P // 4], axis=AX.XY, op=ALU.max).then_inc(s["flag_max"], 1)
            eng.wait_ge(s["flag_max"], 1)
            v.tensor_scalar(flag[0:1, :], flag_f[0:1, :], 1.0, None, ALU.min).then_inc(s["flag_ready"], 1)

        def dve_wq(eng):
            eng.wait_ge(s["g_in_in"], 16)
            eng.wait_ge(s["wq_in"], 16)
            for c in range(DC):
                nc.vector.tensor_scalar(wq[:, c, :], wq[:, c, :], g_in[:, c:c + 1], -SCALE, ALU.mult, ALU.mult).then_inc(s["wq_scaled"], 1)

        def dve_bias(eng):
            eng.wait_ge(s["bias_in"], 16)
            nc.vector.tensor_scalar(bias_late, bias_late, -1.0, None, ALU.mult).then_inc(s["bias_neg"], 1)

        def dve_mask_late(eng):
            eng.wait_ge(s["mask_late_in"], 16)
            nc.vector.tensor_scalar(mask_late, mask_late_raw, -FAR, FAR, ALU.mult, ALU.add).then_inc(s["mask_ready"], 1)

        def dve_null_q(eng):
            for c in range(DC):
                eng.wait_ge(s["wqk_ready"], c + 1)
                nc.vector.tensor_reduce(wvn[:, c, DH:DH + H], wqk[:, c, :, :], axis=AX.X, op=ALU.add).then_inc(s["null_q_ready"], 1)
            eng.wait_ge(s["small_in"], SMALL)

        def dve_wcat(eng):
            v = nc.vector
            v.tensor_copy(null_ctx[:, :], null_vt[:, 0:1].to_broadcast((P, P))).then_inc(s["null_ctx_ready"], 1)
            for c, bk in enumerate((o_bank, f_bank)):
                eng.wait_ge(s[f"ffn_ps{c}"], 1)
                v.tensor_scalar(wcat[:, c, 0:D + E * R], bk[:, 0:D + E * R], g_out[:, c:c + 1], None, ALU.mult)
                v.tensor_scalar(wcat[:, c, D + E * R:], bk[:, D + E * R:FW], g_out[:, c:c + 1], -1.0, ALU.mult, ALU.mult).then_inc(s["wcat_ready"], 1)

        def dve_vcat(eng):
            eng.wait_ge(s["vcat_ps"], 1)
            nc.vector.tensor_scalar(vcat[:, :], o_bank[:, 0:D], 1.0 / R, None, ALU.mult).then_inc(s["vcat_ready"], 1)

        def dve_wo_sum(eng):
            eng.wait_ge(s["wo_in"], 16)
            nc.vector.tensor_reduce(wo_sum, wo[:, :, :].rearrange("p m n -> p n m"), axis=AX.X, op=ALU.add).then_inc(s["wo_sum_ready"], 1)

        def dve_general_setup(eng):
            v = nc.vector
            dve_wq(eng)
            dve_bias(eng)
            dve_null_q(eng)
            v.memset(mask_room[:, :], 0.0).then_inc(s["mask_zero"], 1)
            eng.wait_ge(s["mask_zero"], 1)
            v.tensor_scalar(mask_far[0:1, :, :], mask_row[:, :, :], -FAR, FAR, ALU.mult, ALU.add).then_inc(s["mask_ready"], 1)
            for k in range(2):
                eng.wait_ge(s[f"x_late_in{k}"], 16)
            eng.wait_ge(s["x_rest_in"], 16 * B)

        def dve_general_bias(eng):
            for j in range(QT):
                eng.wait_ge(s[f"bias_in{j}"], 16)
                nc.vector.tensor_scalar(bias_all[j], bias_all[j], -1.0, None, ALU.mult).then_inc(s["bias_neg"], 1)

        def dve_stats(eng, L, r, g):
            v = nc.vector
            ts = L.groups[g]
            if L.late:
                eng.wait_ge(s[f"x_late_in{ts[0] // PART}"], 16)
            for t in ts:
                xin = x_all[:, t, QT - 1, :] if L.late else x_all[:, r, t, :]
                v.bn_stats(stat[:, t, :], xin).then_inc(s["stats_done"], 1)
            for t in ts:
                eng.wait_ge(s["stats_done"], at(r, L.tiles, t + 1))
                held(eng, r)
                v.bn_aggr(mv[:, t, :], stat[:, t, :]).then_inc(s["mv_done"], 1)
            eng.wait_ge(s["mv_done"], at(r, L.tiles, ts[-1] + 1))
            v.tensor_scalar(mv[:, ts[0]:ts[-1] + 1, 1], mv[:, ts[0]:ts[-1] + 1, 1], EPS, None, ALU.add).then_inc(s["var_done"], 1)

        def dve_norm(eng, L, r, g):
            v = nc.vector
            eng.wait_ge(s["rstd_done"], at(r, len(L.groups), g + 1))
            for t in L.groups[g]:
                xin = x_all[:, t, QT - 1, :] if L.late else x_all[:, r, t, :]
                v.tensor_scalar(xn_of(L, t), xin, mv[:, t, 0:1], rstd[:, t:t + 1], ALU.subtract, ALU.mult).then_inc(s["xn_done"], 1)

        def dve_rows(eng, L, r, p):
            eng.wait_ge(s["xnt_ps"], at(r, 2 * L.preps, 2 * p + 1))
            nc.vector.tensor_copy(xn_t_of(p)[:, 0, :], xn_banks[0][:, :]).then_inc(s["xnt_dve"], 1)

        def dve_project(eng, L, r, p, between=()):
            v = nc.vector
            for m in range(1, MC - (len(L.early_queries) if p == L.preps - 1 else 0), 2):
                dve_query(eng, L, r, p, m)
                if m // 2 < len(between):
                    between[m // 2](eng)
                if p and m == MC // 2 - 1:
                    dve_values(eng, L, r, p)
            if p == 0:
                dve_values(eng, L, r, p)

        def dve_query(eng, L, r, p, m):
            eng.wait_ge(s["q_ps"], at(r, MC * L.preps, MC * p + m + 1))
            nc.vector.tensor_copy(q_of(p)[:, m, :], q_banks[m % 4][:, :]).then_inc(s["q_dve"], 1)

        def dve_values(eng, L, r, p):
            v = nc.vector
            eng.wait_ge(s["v_ps"], at(r, L.preps, p + 1))
            both = c_bank[1][:, 0:PART * (DH + H)].rearrange("p (j n) -> p j n", j=PART)
            v.tensor_copy(v_all[:, p, :, :], both[:, :, 0:DH])
            v.tensor_tensor(ns_all[:, p, :, :], both[:, :, DH:], null_bias[:, None, :].to_broadcast((P, PART, H)),
                            ALU.subtract).then_inc(s["v_done"], 1)

        def dve_late_start(eng):
            dve_stats(eng, LATE, 0, 0)
            dve_stats(eng, LATE, 0, 1)
            dve_norm(eng, LATE, 0, 0)
            dve_norm(eng, LATE, 0, 1)
            dve_rows(eng, LATE, 0, 0)
            dve_wq(eng)
            dve_stats(eng, LATE, 0, 2)
            dve_norm(eng, LATE, 0, 2)
            dve_project(eng, LATE, 0, 0, (dve_null_q, lambda e: (dve_rows(e, LATE, 0, 1), dve_mask_late(e)), dve_bias))
            dve_wcat(eng)
            dve_project(eng, LATE, 0, 1, (dve_wo_sum, dve_vcat))

        def dve_rest(eng, b):
            if b == 0:
                eng.wait_ge(s["f_read"], f_use(LATE, ("lora", -1, 0)) + 1)
                eng.wait_ge(s["x_rest_in"], 16 * B)
            part = x_all[:, b, 0:QT - 1, :]
            nc.vector.tensor_tensor(part, part, y_null[:, None, :].to_broadcast((P, QT - 1, D)),
                                    ALU.add).then_inc(s["rest_done"], 1)

        def dve_round(eng, L, r):
            v = nc.vector

            def gate_max(t, k):
                batch = L.batches[k]
                eng.wait_ge(s["lora_in_done"], at(r, L.sides, L.first_side + t + 1))
                v.tensor_reduce(gate_1[:, 0, slots(batch)], lora_in_of(L, batch[0], len(batch))[:, :, E * R:],
                                axis=AX.X, op=ALU.min).then_inc(s["gmax_done"], 1)

            for n in range(L.steps):
                for name, t, hf in sorted(L.at(n), key=lambda x: x[0] != "norm"):
                    k = t + L.first_side
                    if name == "norm":
                        eng.wait_ge(s["orstd_done"], at(r, L.sides, k + 1))
                        v.tensor_scalar(xt[:, :], o_of(L, t)[:, 0:D], omv[:, 0:1], orstd[:, 0:1],
                                        ALU.subtract, ALU.mult).then_inc(s["xt_done"], 1)
                    if name == "base":
                        bk, ps, read, per, use = f_of(L, ("ffn", t, 0))
                        eng.wait_ge(ps, at(r, per, use + 1))
                        v.tensor_copy(lora_in_of(L, t, 1)[:, 0, :], bk[:, D:FW]).then_inc(s["lora_in_done"], 1)
                        if t < 0:
                            v.tensor_copy(y_null[:, :], bk[:, 0:D]).then_inc(read, 1)
                        else:
                            row = x_all[:, t, QT - 1, :] if L.late else x_all[:, r, t, :]
                            if L.late and t == L.tiles - 1:
                                gate_max(t, len(L.batches) - 1)
                            v.tensor_tensor(row, bk[:, 0:D], row, ALU.add).then_inc(read, 1)
                    if name == "fin":
                        kb, pair = L.pairs[hf]
                        use = f_use(L, ("lora", t, hf))
                        _, _, read, per, base = f_of(L, ("ffn", pair[-1], 0))
                        eng.wait_ge(read, at(r, per, base + 1))
                        eng.wait_ge(s["f_ps"], at(r, len(L.f_uses), use + 1))
                        t0, nt = pair[0], len(pair)
                        if t0 < 0:
                            row = y_null[:, None, :]
                        else:
                            row = x_all[:, t0:t0 + nt, QT - 1, :] if L.late else x_all[:, r, t0:t0 + nt, :]
                        v.tensor_tensor(row, f_bank[:, 0:nt * D].rearrange("p (b d) -> p b d", b=nt), row, ALU.add).then_inc(s["f_read"], 1)
                if n < L.nu:
                    t, h0, per = L.units[n]
                    nk = L.nk[t]
                    if n >= 3:
                        eng.wait_ge(s["t_ps"], at(r, L.nu, n - 2))
                    if n == 0:
                        eng.wait_ge(s["v_done"], at(r, L.preps, L.preps))
                        if not L.late:
                            eng.wait_ge(s["bias_ready"], 1 + QT)
                    if L.late:
                        eng.wait_ge(s["bias_masked_ready"], n + 1)
                    eng.wait_ge(s["s_ps"], at(r, L.nu, n + 1))
                    held(eng, r)
                    for i in range(per):
                        h = h0 + i
                        bias = bias_masked[:, t % 2, h, :] if L.late else bias_all[t][:, h, :]
                        last = v.tensor_tensor_reduce(
                            out=probs[:, n % 3, i * nk:(i + 1) * nk], in0=s_bank[n % 2][:, i * nk:(i + 1) * nk],
                            in1=bias, scale=1.0, scalar=ns_all[:, t // PART, t % PART, h:h + 1], op0=ALU.add,
                            op1=ALU.min, accum_out=neg_max[:, t % 2, h:h + 1])
                    last.then_inc(s["scores_done"], 1)
                for name, t, hf in L.at(n):
                    i, k, piece = 2 * t + hf, t + L.first_side, (name, t, hf)
                    hs = slice(8 * hf, 8 * hf + 8)
                    if name == "query" and hf % 2:
                        dve_query(eng, L, r, L.preps - 1, hf)
                    if name == "delta":
                        eng.wait_ge(s["scores_done"], at(r, L.nu, L.last_unit[t, hf] + 1))
                        v.tensor_tensor(small[:, 0, hf, :], neg_max[:, t % 2, hs], ns_all[:, t // PART, t % PART, hs],
                                        ALU.subtract).then_inc(s["delta_done"], 1)
                    if name == "den":
                        eng.wait_ge(s["p0_done"], at(r, 2 * L.tiles, i + 1))
                        eng.wait_ge(s["exp_done"], at(r, L.nu, L.last_unit[t, hf] + 1))
                        v.tensor_tensor(small[:, 2, hf, :], small[:, 1, hf, :], sums[:, t % 2, hs], ALU.add).then_inc(s["den_done"], 1)
                        eng.wait_ge(s["den_done"], at(r, 2 * L.tiles, i + 1))
                        v.reciprocal(small[:, 4, hf, :], small[:, 2, hf, :]).then_inc(s["rden_done"], 1)
                        eng.wait_ge(s["rden_done"], at(r, 2 * L.tiles, i + 1))
                        v.tensor_tensor(small[:, 3, hf, :], small[:, 1, hf, :], small[:, 4, hf, :], ALU.mult).then_inc(s["p0n_done"], 1)
                    if name == "ctx":
                        eng.wait_ge(s["pv_done"], at(r, L.nu, L.last_unit[t, hf] + 1))
                        if t:
                            eng.wait_ge(s["x_ps"], at(r, len(L.x_uses), x_use(L, ("turn", t - 1, hf)) + 1))
                        v.tensor_tensor(attn[:, hf, :].rearrange("p (h e) -> p h e", h=8),
                                        c_bank[hf][:, :].rearrange("p (h e) -> p h e", h=8),
                                        small[:, 4, hf, :].unsqueeze(2).to_broadcast((P, 8, DH)), ALU.mult).then_inc(s["attn_mul_done"], 1)
                    if name == "stat":
                        eng.wait_ge(s["o_ps"], at(r, L.sides, k + 1))
                        v.bn_stats(ostat[:, :], o_of(L, t)[:, 0:D]).then_inc(s["ostat_done"], 1)
                        eng.wait_ge(s["ostat_done"], at(r, L.sides, k + 1))
                        held(eng, r)
                        v.bn_aggr(omv[:, :], ostat[:, :]).then_inc(s["omv_done"], 1)
                        eng.wait_ge(s["omv_done"], at(r, L.sides, k + 1))
                        v.tensor_scalar(omv[:, 1:2], omv[:, 1:2], EPS, None, ALU.add).then_inc(s["ovar_done"], 1)
                    if name == "gmax" and not (L.late and t == L.tiles - 1):
                        gate_max(t, hf)
                    if name == "gate":
                        batch = L.batches[hf]
                        bs, lin = slots(batch), lora_in_of(L, batch[0], len(batch))
                        eng.wait_ge(s["gexp_done"], at(r, len(L.batches), hf + 1))
                        v.reciprocal(gate_1[:, 2, bs], gate_1[:, 1, bs]).then_inc(s["grec_done"], 1)
                        eng.wait_ge(s["grec_done"], at(r, len(L.batches), hf + 1))
                        for b in range(len(batch)):
                            b1 = bs.start + b
                            last = v.scalar_tensor_tensor(tg[:, b1, :].rearrange("p (e q) -> p e q", e=E),
                                                          lin[:, b, 0:E * R].rearrange("p (e q) -> p e q", e=E), gate_1[:, 2, b1:b1 + 1],
                                                          gate_e[:, b1, :].unsqueeze(2).to_broadcast((P, E, R)), ALU.mult, ALU.mult)
                        last.then_inc(s["tg_done"], 1)

                if L.late and 12 <= n < 12 + B:
                    dve_rest(eng, n - 12)

        def act_warm(eng):
            eng.wait_ge(s["ident_ready"], 1)
            nc.scalar.activation(sums[:, 0, 0:1], ident[:, 0:1], ACT.Exp).then_inc(s["table_in"], 1)

        def act_wkv(eng):
            a = nc.scalar
            eng.wait_ge(s["g_in_in"], 16)
            eng.wait_ge(s["wkv_in"], 16)
            for c in range(DC):
                for to, start in ((wkk[:, c, 0:DH], 0), (wkk[:, c, DH:P], 0), (wvn[:, c, 0:DH], DH)):
                    last = a.activation(to, wkv_raw[:, c, start:start + DH], ACT.Copy, scale=g_in[:, c:c + 1])
            last.then_inc(s["wkk_ready"], 1)

        def act_round(eng, L, r):
            a = nc.scalar
            def rows(p):
                eng.wait_ge(s["xnt_ps"], at(r, 2 * L.preps, 2 * p + 2))
                a.activation(xn_t_of(p)[:, 1, :], xn_banks[1][:, :], ACT.Copy).then_inc(s["xnt_act"], 1)

            def query(p, m):
                eng.wait_ge(s["q_ps"], at(r, MC * L.preps, MC * p + m + 1))
                a.activation(q_of(p)[:, m, :], q_banks[m % 4][:, :], ACT.Copy).then_inc(s["q_act"], 1)

            rows(0)
            for p in range(L.preps):
                eng.wait_ge(s["k_ps"], at(r, L.preps, p + 1))
                a.activation(kt_of(p)[0:DH, 0, :], c_bank[0][0:DH, :], ACT.Copy)
                a.activation(kt_of(p)[DH:P, 1, :], c_bank[0][DH:P, :], ACT.Copy).then_inc(s["kt_done"], 1)
                for m in range(0, MC - (len(L.early_queries) if p == L.preps - 1 else 0), 2):
                    query(p, m)
                    if m == 2 and p + 1 < L.preps:
                        rows(p + 1)

            for n in range(L.steps):
                for piece in L.at(n - 1):
                    name, t, hf = piece
                    if name == "xtt":
                        bk, ps, read, per, use = f_of(L, piece)
                        eng.wait_ge(ps, at(r, per, use + 1))
                        a.activation(xt_t[:, :, :], bk[:, 0:D].rearrange("p (c q) -> p c q", c=DC), ACT.Copy).then_inc(read, 1)
                    if name in ("turn", "tgt"):
                        eng.wait_ge(s["x_ps"], at(r, len(L.x_uses), x_use(L, piece) + 1))
                        if name == "turn":
                            to, w = attn_t[:, 4 * hf:4 * hf + 4, :], 4
                        else:
                            w = len(L.batches[hf])
                            to = tg_t[:, slots(L.batches[hf]), :]
                        a.activation(to, x_bank[:, 0:w * P].rearrange("p (m q) -> p m q", m=w), ACT.Copy).then_inc(s["x_read"], 1)
                if 2 <= n < L.nu + 2:
                    u = n - 2
                    w = L.units[u][2] * L.nk[L.units[u][0]]
                    if u >= 2:
                        eng.wait_ge(s["pv_done"], at(r, L.nu, u - 1))
                    eng.wait_ge(s["t_ps"], at(r, L.nu, u + 1))
                    a.activation(probs_t[:, u % 2, 0:w], t_bank[:, 0:w], ACT.Copy).then_inc(s["probs_t_done"], 1)
                if n < L.nu:
                    t, h0, per = L.units[n]
                    nk = L.nk[t]
                    eng.wait_ge(s["scores_done"], at(r, L.nu, n + 1))
                    for i in range(per):
                        h = h0 + i
                        slot = probs[:, n % 3, i * nk:(i + 1) * nk]
                        last = a.activation(slot, slot, ACT.Exp, bias=neg_max[:, t % 2, h:h + 1], scale=-1.0,
                                            accum_out=sums[:, t % 2, h:h + 1])
                    last.then_inc(s["exp_done"], 1)
                for name, t, hf in L.at(n):
                    i, k, piece = 2 * t + hf, t + L.first_side, (name, t, hf)
                    if name == "query" and hf % 2 == 0:
                        query(L.preps - 1, hf)
                    if name == "p0":
                        eng.wait_ge(s["delta_done"], at(r, 2 * L.tiles, i + 1))
                        a.activation(small[:, 1, hf, :], small[:, 0, hf, :], ACT.Exp).then_inc(s["p0_done"], 1)
                    if name == "gexp":
                        batch = L.batches[hf]
                        lin = lora_in_of(L, batch[0], len(batch))
                        eng.wait_ge(s["gmax_done"], at(r, len(L.batches), hf + 1))
                        for b in range(len(batch)):
                            b1 = slots(batch).start + b
                            last = a.activation(gate_e[:, b1, :], lin[:, b, E * R:], ACT.Exp, bias=gate_1[:, 0, b1:b1 + 1],
                                                scale=-1.0, accum_out=gate_1[:, 1, b1:b1 + 1])
                        last.then_inc(s["gexp_done"], 1)

        def pe_warm(eng):
            eng.wait_ge(s["ident_ready"], 1)
            for _ in range(WARM):
                nc.tensor.matmul(t_bank[:, 0:P], ident[:, :], ident[:, :], start=True, stop=True)

        def pe_wcat(eng, L):
            pe = nc.tensor
            eng.wait_ge(s["ffn_in"], 16 * 5)
            eng.wait_ge(s["xnt_dve"], L.preps)
            eng.wait_ge(s["xnt_act"], L.preps)
            for c, bk in enumerate((o_bank, f_bank)):
                cols = slice(c * P, (c + 1) * P)
                for o2 in range(2):
                    pe.transpose(bk[:, o2 * P:(o2 + 1) * P], w_raw[:, o2, cols], ident[:, :])
                pe.transpose(bk[:, D:D + P], u_raw[:, cols], ident[:, :])
                pe.transpose(bk[:, D + P:FW], gate_raw[0:E, cols], ident[0:E, 0:E]).then_inc(s[f"ffn_ps{c}"], 1)

        def pe_vcat(eng):
            pe = nc.tensor
            eng.wait_ge(s["wcat_ready"], 1)
            pe.transpose(o_bank[:, 0:P], v_raw[:, 0, :], ident[:, :])
            pe.transpose(o_bank[:, P:D], v_raw[:, 1, :], ident[:, :]).then_inc(s["vcat_ps"], 1)

        def pe_turn_rows(eng, L, r, p):
            pe = nc.tensor
            if p:
                eng.wait_ge(s["xnt_dve"], at(r, L.preps, p))
                eng.wait_ge(s["xnt_act"], at(r, L.preps, p))
            for c in range(DC):
                for j in range(PART):
                    if c == 0:
                        eng.wait_ge(s["xn_done"], at(r, L.tiles, PART * p + j + 1))
                    last = pe.transpose(xn_banks[c][:, j * P:(j + 1) * P], xn_of(L, PART * p + j)[:, c * P:(c + 1) * P], ident[:, :])
                last.then_inc(s["xnt_ps"], 1)

        def pe_keys(eng, L, r, p, first):
            if first and p == 0:
                eng.wait_ge(s["wkk_ready"], 1)
            if p:
                eng.wait_ge(s["kt_done"], at(r, L.preps, p))
            for c, half_in in enumerate(("xnt_dve", "xnt_act")):
                eng.wait_ge(s[half_in], at(r, L.preps, p + 1))
                last = nc.tensor.matmul(c_bank[0][:, :], wkk[:, c, :], xn_t_of(p)[:, c, :], start=(c == 0), stop=(c == DC - 1))
            last.then_inc(s["k_ps"], 1)

        def pe_queries(eng, L, r, p, ms, first):
            for m in ms:
                if m >= 4 or p:
                    eng.wait_ge(s["q_dve" if m % 2 else "q_act"], at(r, 4 * L.preps, 4 * p + m // 2 - 1))
                for c in range(DC):
                    if first and p == 0 and m == 0:
                        eng.wait_ge(s["wq_scaled"], c + 1)
                    last = nc.tensor.matmul(q_banks[m % 4][:, :], wq[:, c, m * P:(m + 1) * P], xn_t_of(p)[:, c, :],
                                            start=(c == 0), stop=(c == DC - 1))
                last.then_inc(s["q_ps"], 1)

        def pe_values(eng, L, r, p, first):
            if first and p == 0:
                eng.wait_ge(s["null_q_ready"], DC)
            if p:
                eng.wait_ge(s["v_done"], at(r, L.preps, p))
            for j in range(PART):
                for c in range(DC):
                    last = nc.tensor.matmul(c_bank[1][:, j * (DH + H):(j + 1) * (DH + H)], xn_t_of(p)[:, c, j * P:(j + 1) * P],
                                            wvn[:, c, :], start=(c == 0), stop=(c == DC - 1))
            last.then_inc(s["v_ps"], 1)

        def pe_project(eng, L, r, first):
            pe_turn_rows(eng, L, r, 0)
            for p in range(L.preps):
                later = L.early_queries if p == L.preps - 1 else ()
                pe_keys(eng, L, r, p, first)
                pe_queries(eng, L, r, p, range(MC // 2), first)
                if p + 1 < L.preps:
                    pe_turn_rows(eng, L, r, p + 1)
                if p:
                    if first:
                        pe_vcat(eng)
                    pe_values(eng, L, r, p, first)
                pe_queries(eng, L, r, p, range(MC // 2, MC - len(later)), first)
                if p == 0:
                    pe_values(eng, L, r, p, first)
                    if first:
                        pe_wcat(eng, L)
            if first and not L.late:
                pe_vcat(eng)

        def pe_round(eng, L, r, first):
            pe = nc.tensor
            eng.wait_ge(s["q_act"], at(r, 4 * L.preps, 4 * L.preps - 1))
            eng.wait_ge(s["q_dve"], at(r, 4 * L.preps, 4 * L.preps - 1))
            eng.wait_ge(s["kt_done"], at(r, L.preps, L.preps))
            eng.wait_ge(s["v_done"], at(r, L.preps, L.preps))
            if first:
                if not L.late:
                    eng.wait_ge(s["mask_ready"], 1)
                eng.wait_ge(s["consts_ready"], 2)
                eng.wait_ge(s["null_ctx_ready"], 1)
                eng.wait_ge(s["vcat_ready"], 1)
                eng.wait_ge(s["wcat_ready"], 2)
                eng.wait_ge(s["wo_in"], 16)

            def free_x(piece):
                if x_use(L, piece):
                    eng.wait_ge(s["x_read"], at(r, len(L.x_uses), x_use(L, piece)))

            def free_f(piece):
                bk, ps, read, per, use = f_of(L, piece)
                if use:
                    eng.wait_ge(read, at(r, per, use))
                return bk, ps

            for n in range(L.steps):
                if n < L.nu:
                    t, h0, per = L.units[n]
                    nk, k0, p, j = L.nk[t], L.k0[t], t // PART, t % PART
                    bk = s_bank[n % 2]
                    if n >= 2:
                        eng.wait_ge(s["scores_done"], at(r, L.nu, n - 1))
                    if not L.late:
                        pe.matmul(bk[:, 0:per * nk], pick[:, :], mask_far[:, r, 0:nk].unsqueeze(1).to_broadcast((P, per, nk)),
                                  start=True, stop=False)
                    if per == 1:
                        last = pe.matmul(bk[:, 0:nk], q_of(p)[:, h0 // 2, j * P:(j + 1) * P],
                                         kt_of(p)[:, h0 % 2, k0:k0 + nk], start=False, stop=True)
                    else:
                        for i in range(0, per, 2):
                            last = pe.matmul(bk[:, i * nk:(i + 2) * nk].rearrange("p (e k) -> p e k", e=2),
                                             q_of(p)[:, (h0 + i) // 2, j * P:(j + 1) * P],
                                             kt_of(p)[:, :, k0:k0 + nk], start=L.late, stop=(L.late or i == per - 2))
                    last.then_inc(s["s_ps"], 1)
                if 2 <= n < L.nu + 2:
                    u = n - 2
                    t, h0, per = L.units[u]
                    if u == 0:
                        eng.wait_ge(s["q_act"], at(r, 4 * L.preps, 4 * L.preps))
                        eng.wait_ge(s["q_dve"], at(r, 4 * L.preps, 4 * L.preps))
                    if u >= 1:
                        eng.wait_ge(s["probs_t_done"], at(r, L.nu, u))
                    eng.wait_ge(s["exp_done"], at(r, L.nu, u + 1))
                    for i in range(per * L.nk[t] // P):
                        last = pe.transpose(t_bank[:, i * P:(i + 1) * P], probs[:, u % 3, i * P:(i + 1) * P], ident[:, :])
                    last.then_inc(s["t_ps"], 1)
                if 3 <= n < L.nu + 3:
                    u = n - 3
                    t, h0, per = L.units[u]
                    nb = L.nk[t] // P
                    if h0 % 8 == 0 and t:
                        eng.wait_ge(s["attn_mul_done"], at(r, 2 * L.tiles, 2 * (t - 1) + h0 // 8 + 1))
                    eng.wait_ge(s["probs_t_done"], at(r, L.nu, u + 1))
                    for i in range(per):
                        h = h0 + i
                        for kb in range(nb):
                            last = pe.matmul(c_bank[h // 8][:, (h % 8) * DH:(h % 8 + 1) * DH],
                                             probs_t[:, u % 2, (i * nb + kb) * P:(i * nb + kb + 1) * P],
                                             v_all[:, t // PART, L.k0[t] // P + kb, :], start=(kb == 0), stop=(kb == nb - 1))
                    last.then_inc(s["pv_done"], 1)
                for name, t, hf in L.at(n):
                    i, k, piece = 2 * t + hf, t + L.first_side, (name, t, hf)
                    if name == "query":
                        pe_queries(eng, L, r, L.preps - 1, (hf,), False)
                    if name == "turn":
                        free_x(piece)
                        eng.wait_ge(s["attn_done"], at(r, 2 * L.tiles, i + 1))
                        for m in range(4):
                            last = pe.transpose(x_bank[:, m * P:(m + 1) * P], attn[:, hf, m * P:(m + 1) * P], ident[:, :])
                        last.then_inc(s["x_ps"], 1)
                    if name in ("out", "out_end"):
                        if t >= 0:
                            eng.wait_ge(s["x_read"], at(r, len(L.x_uses), x_use(L, ("turn", t, name == "out_end")) + 1))
                        if name == "out" and t == L.tiles - 1:
                            eng.wait_ge(s["scores_done"], at(r, L.nu, L.nu))
                        elif name == "out" and k:
                            eng.wait_ge(s["xt_done"], at(r, L.sides, k))
                        if t < 0:
                            ms = ()
                            if name == "out_end":
                                eng.wait_ge(s["wo_sum_ready"], 1)
                                last = pe.matmul(o_bank[:, 0:D], null_ctx[:, :], wo_sum, start=True, stop=True)
                        else:
                            ms = range(4) if name == "out" else range(4, MC)
                        for m in ms:
                            last = pe.matmul(o_of(L, t)[:, 0:D], attn_t[:, m, :], wo[:, m, :], start=(m == 0), stop=(m == MC - 1))
                        if name == "out_end":
                            last.then_inc(s["o_ps"], 1)
                    if name == "xtt":
                        bk, ps = free_f(piece)
                        eng.wait_ge(s["xt_done"], at(r, L.sides, k + 1))
                        for c in range(DC):
                            last = pe.transpose(bk[:, c * P:(c + 1) * P], xt[:, c * P:(c + 1) * P], ident[:, :])
                        last.then_inc(ps, 1)
                    if name == "ffn":
                        bk, ps = free_f(piece)
                        for c in range(DC):
                            last = pe.matmul(bk[:, 0:FW], xt_t[:, c, :], wcat[:, c, :], start=(c == 0), stop=(c == DC - 1))
                        last.then_inc(ps, 1)
                    if name == "tgt":
                        free_x(piece)
                        eng.wait_ge(s["tg_done"], at(r, len(L.batches), hf + 1))
                        for b in range(len(L.batches[hf])):
                            last = pe.transpose(x_bank[:, b * P:(b + 1) * P], tg[:, slots(L.batches[hf]).start + b, :], ident[:, :])
                        last.then_inc(s["x_ps"], 1)
                    if name == "lora":
                        kb, pair = L.pairs[hf]
                        free_f(piece)
                        eng.wait_ge(s["x_read"], at(r, len(L.x_uses), x_use(L, ("tgt", t, kb)) + 1))
                        for b, tile in enumerate(pair):
                            last = pe.matmul(f_bank[:, b * D:(b + 1) * D], tg_t[:, max(tile, 0) % PART, :], vcat[:, :],
                                             start=True, stop=True)
                        last.then_inc(s["f_ps"], 1)

        LATE, ALL = Layout(True), Layout(False)

        def sp_general_bias(eng):
            eng.wait_ge(s["bias_ready"], 1)
            eng.wait_ge(s["vcat_ready"], 1)
            eng.wait_ge(s["null_q_ready"], DC)
            eng.wait_ge(s["mask_late_in"], 16)
            eng.wait_ge(s["consts_ready"], 2)
            for j in range(QT):
                eng.dma_start(bias_all[j], bias_d[:, j * P:(j + 1) * P, 0:(j + 1) * P]
                              .rearrange("h p k -> p h k")).then_inc(s[f"bias_in{j}"], 16)

        def sp_round(eng, L, r):
            if L.late:
                for b in range(B):
                    eng.wait_ge(s["rest_done"], b + 1)
                    eng.dma_start(out_d[b, 0:(QT - 1) * P, :].rearrange("(t p) d -> p t d", p=P),
                                  x_all[:, b, 0:QT - 1, :]).then_inc(s["stored"], 16)
            for name, t, hf in L.f_uses:
                if name != "lora" or t < 0:
                    continue
                eng.wait_ge(s["f_read"], at(r, len(L.f_uses), f_use(L, (name, t, hf)) + 1))
                t0, nt = L.pairs[hf][1][0], len(L.pairs[hf][1])
                if L.late:
                    eng.dma_start(out_d[t0:t0 + nt, (QT - 1) * P:, :].rearrange("t p d -> p t d"),
                                  x_all[:, t0:t0 + nt, QT - 1, :]).then_inc(s["stored"], 16)
                else:
                    rows = out_d[bass.ds(r, 1), t0 * P:(t0 + nt) * P, :]
                    eng.dma_start(rows.rearrange("a (t p) d -> p (a t) d", p=P),
                                  x_all[:, r, t0:t0 + nt, :]).then_inc(s["stored"], 16)

        def paths(eng, late, general, body, finish=lambda L: None):
            eng.wait_ge(s["flag_ready"], 1)
            early = eng.value_load(flag[0:1, 0:1], min_val=0, max_val=1)
            with eng.If(early == 0):
                late()
                body(LATE, 0, True)
                finish(LATE)
            with eng.Else():
                general()
                body(ALL, 0, True)
                with eng.Fori(1, B) as r:
                    body(ALL, r, False)
                finish(ALL)

        def nothing():
            pass

        @block.sync
        def _(sp):
            sp_setup(sp)
            paths(sp, nothing, lambda: sp_general_bias(sp), lambda L, r, first: sp_round(sp, L, r),
                  lambda L: sp.wait_ge(s["stored"], 16 * (B + sum(p[0] >= 0 for _, p in L.pairs) if L.late else B * len(L.pairs))))

        @block.gpsimd
        def _(pool):
            pool_setup(pool)
            paths(pool, lambda: pool_late_start(pool), lambda: pool_null_key(pool),
                  lambda L, r, first: (
                      None if L.late else (pool_rstd(pool, L, r, 0), pool_general_bias(pool) if first else None),
                      pool_round(pool, L, r)))

        @block.scalar
        def _(act):
            act_setup_dma(act)
            act_warm(act)
            paths(act, lambda: act_wkv(act), lambda: act_wkv(act), lambda L, r, first: act_round(act, L, r))

        @block.vector
        def _(dve):
            dve_flag(dve)
            paths(dve, lambda: dve_late_start(dve), lambda: dve_general_setup(dve), lambda L, r, first: (
                None if L.late else (dve_stats(dve, L, r, 0), dve_norm(dve, L, r, 0),
                                     dve_rows(dve, L, r, 0), dve_project(dve, L, r, 0),
                                     (dve_wcat(dve), dve_vcat(dve), dve_general_bias(dve)) if first else None),
                dve_round(dve, L, r)))

        @block.tensor
        def _(pe):
            pe_warm(pe)
            paths(pe, nothing, nothing, lambda L, r, first: (
                pe_project(pe, L, r, first), pe_round(pe, L, r, first)))


_INS = ["x", "fside_16xSxS_0", "cond_64", "mask_BxS_bk0", "L0_cond_g_in", "L0_cond_null_attn_bias", "L0_cond_Wq",
        "L0_cond_Wkv", "L0_cond_Wo", "L0_cond_g_out", "L0_ffn_weight", "L0_ffn_gate_w", "L0_ffn_lora_U",
        "L0_ffn_lora_V"]


def kernel(**inputs):
    import numpy as np
    import concourse.bacc as bacc
    from concourse import mybir as mb
    from concourse.bass_utils import run_bass_kernel_spmd

    nc = bacc.Bacc("TRN2", target_bir_lowering=False, num_devices=1)
    arrays, args = {}, []
    for name in _INS:
        a = np.ascontiguousarray(inputs[name])
        arrays[f"in_{name}"] = a
        args.append(nc.dram_tensor(f"in_{name}", a.shape, mb.dt.from_np(a.dtype), kind="ExternalInput").ap())
    args.append(nc.dram_tensor("out", (B, N, D), mb.dt.float32, kind="ExternalOutput").ap())
    attention_ffn(nc, *args)
    r = run_bass_kernel_spmd(nc, [arrays], core_ids=[0])
    return r.results[0]["out"]
```
